# Optimizing a Trainium2 kernel written in Bass

```python
import numpy as np
import jax
import jax.numpy as jnp

def _softmax(x, axis=-1):
    return jax.nn.softmax(x, axis=axis)

def _gelu(x):
    return jax.nn.gelu(x, approximate=True)

def _silu(x):
    return jax.nn.silu(x)

def _sigmoid(x):
    return jax.nn.sigmoid(x)

def _layernorm(x, axis=-1, eps=1e-05):
    m = jnp.mean(x, axis=axis, keepdims=True)
    v = jnp.var(x, axis=axis, keepdims=True)
    return (x - m) / jnp.sqrt(v + eps)

def _scatter_add(tgt, idx, src, axis=0):
    return tgt.at[idx].add(src)

def _segment_sum(src, seg, n):
    return jax.ops.segment_sum(src, seg, n)
kernel_name = 'mk_seq_preln_d1_jaxref_r8_dae108'

def setup_inputs(seed: int=0):
    np.random.seed(seed)
    _w = jnp.asarray

    def _L0_attn_setup():
        import jax, jax.numpy as jnp
        import numpy as np
        HIDDEN = 512
        HEADS = 32
        D_K = HIDDEN // HEADS
        key = jax.random.key(seed)
        ks = jax.random.split(key, 5)
        scale = 1.0 / np.sqrt(HIDDEN)
        x = jax.random.normal(ks[0], (2, 256, HIDDEN), dtype=jnp.float32)
        w_q = jax.random.uniform(ks[1], (HIDDEN, HIDDEN), jnp.float32, -scale, scale)
        w_k = jax.random.uniform(ks[2], (HIDDEN, HIDDEN), jnp.float32, -scale, scale)
        w_v = jax.random.uniform(ks[3], (HIDDEN, HIDDEN), jnp.float32, -scale, scale)
        w_o = jax.random.uniform(ks[4], (HIDDEN, HIDDEN), jnp.float32, -scale, scale)
        return {'x': x, 'w_q': w_q, 'w_k': w_k, 'w_v': w_v, 'w_o': w_o}
    _L0_attn_in = _L0_attn_setup()

    def _L0_ffn_setup():
        import jax, jax.numpy as jnp
        import numpy as np
        H, F, E, K = (512, 800, 8, 2)
        B, S = (1, 64)
        key = jax.random.key(seed)
        k0, k1, k2, k3, k4 = jax.random.split(key, 5)
        x = jax.random.normal(k0, (B, S, H), dtype=jnp.float32)
        gate_w = jax.random.normal(k1, (E, H), dtype=jnp.float32) * 0.02
        w1 = jax.random.normal(k2, (E, F, H), dtype=jnp.float32) * 0.02
        w3 = jax.random.normal(k3, (E, F, H), dtype=jnp.float32) * 0.02
        w2 = jax.random.normal(k4, (E, H, F), dtype=jnp.float32) * 0.02
        return {'x': x, 'gate_w': gate_w, 'w1': w1, 'w2': w2, 'w3': w3}
    _L0_ffn_in = _L0_ffn_setup()
    _d = {'L0_attn_x': _L0_attn_in['x'], 'L0_attn_w_q': _L0_attn_in['w_q'], 'L0_attn_w_k': _L0_attn_in['w_k'], 'L0_attn_w_v': _L0_attn_in['w_v'], 'L0_attn_w_o': _L0_attn_in['w_o'], 'L0_ffn_gate_w': _L0_ffn_in['gate_w'], 'L0_ffn_w1': _L0_ffn_in['w1'], 'L0_ffn_w2': _L0_ffn_in['w2'], 'L0_ffn_w3': _L0_ffn_in['w3']}
    _x0 = _d['L0_attn_x']
    _d['L0_attn_x'] = jax.random.normal(jax.random.fold_in(jax.random.key(seed), 1), (2, 512, 512), dtype=_x0.dtype)
    del _x0
    return _d

def reference(L0_attn_x, L0_attn_w_q, L0_attn_w_k, L0_attn_w_v, L0_attn_w_o, L0_ffn_gate_w, L0_ffn_w1, L0_ffn_w2, L0_ffn_w3):

    def _L0_attn_ref(x, w_q, w_k, w_v, w_o):
        import jax, jax.numpy as jnp
        import numpy as np
        HIDDEN = 512
        HEADS = 32
        D_K = HIDDEN // HEADS
        B, S, _ = x.shape

        def proj(w):
            y = jnp.einsum('bsd,ed->bse', x, w)
            return y.reshape(B, S, HEADS, D_K).transpose(0, 2, 1, 3)
        q, k, v = (proj(w_q), proj(w_k), proj(w_v))
        scores = jnp.einsum('bhqd,bhkd->bhqk', q, k) / jnp.sqrt(jnp.float32(D_K))
        attn = jax.nn.softmax(scores, axis=-1)
        out = jnp.einsum('bhqk,bhkd->bhqd', attn, v)
        out = out.transpose(0, 2, 1, 3).reshape(B, S, HIDDEN)
        return jnp.einsum('bse,oe->bso', out, w_o)

    def _L0_ffn_ref(x, gate_w, w1, w2, w3):
        import jax, jax.numpy as jnp
        import numpy as np
        H, F, E, K = (512, 800, 8, 2)
        B, S = (1, 64)
        b, s, h = x.shape
        xt = x.reshape(-1, h)
        T = xt.shape[0]
        logits = xt @ gate_w.T
        probs = jax.nn.softmax(logits, axis=-1)
        top_vals, top_idx = jax.lax.top_k(probs, K)
        top_vals = top_vals / jnp.sum(top_vals, axis=-1, keepdims=True)
        w_full = jnp.zeros((T, E), dtype=xt.dtype).at[jnp.arange(T)[:, None], top_idx].add(top_vals)
        h1 = jnp.einsum('th,efh->tef', xt, w1)
        h3 = jnp.einsum('th,efh->tef', xt, w3)
        act = jax.nn.silu(h1) * h3
        expert_out = jnp.einsum('tef,ehf->teh', act, w2)
        y = jnp.einsum('te,teh->th', w_full, expert_out)
        return y.reshape(b, s, h)
    x = L0_attn_x
    x = x + _L0_attn_ref(_layernorm(x, axis=-1), L0_attn_w_q, L0_attn_w_k, L0_attn_w_v, L0_attn_w_o)
    x = x + _L0_ffn_ref(_layernorm(x, axis=-1), L0_ffn_gate_w, L0_ffn_w1, L0_ffn_w2, L0_ffn_w3)
    return x

_drawn_inputs = setup_inputs


def setup_inputs(seed=0):
    import zlib

    import numpy as np

    out = dict(_drawn_inputs(seed))
    spreads = {}
    factors = {'L0_attn_w_q': 5.831,
     'L0_attn_w_k': 4.907,
     'L0_attn_w_v': 3.023,
     'L0_attn_w_o': 3.0,
     'L0_ffn_gate_w': 3.956,
     'L0_ffn_w1': 3.502,
     'L0_ffn_w2': 3.421,
     'L0_ffn_w3': 3.413}
    for name, (base, spread) in spreads.items():
        noise = np.random.default_rng([zlib.crc32(name.encode()), seed]).standard_normal(out[name].shape)
        drawn = base * np.exp(spread * noise) if base else spread * noise
        out[name] = jnp.asarray(drawn.astype(out[name].dtype))
    for name, factor in factors.items():
        out[name] = (out[name] * factor).astype(out[name].dtype)
    return out
```

```python
import concourse.bass as bass
from concourse import mybir
from contextlib import ExitStack

P = 128
B, S, HID = 2, 512, 512
NH, D = 32, 16
T = B * S
NT = T // P
TPB = S // P
HC = HID // P
E, F, TOPK = 8, 800, 2
FH = F // 2
FC = -(-F // P)
FTAIL = F - (FC - 1) * P
GH = 4
NG = B * NH // GH
UNITS = 8
PROD = 3
ROWS = PROD * D
RING = 4
MT = (T * TOPK - E) // P + E
EPS = 1e-5


def moe_layer(nc: bass.Bass, x, wq, wk, wv, wo, gw, w13, w2, w2t, out):
    f32, f32r, bf16 = mybir.dt.float32, mybir.dt.float32r, mybir.dt.bfloat16
    i32, u32 = mybir.dt.int32, mybir.dt.uint32
    ALU, ACT, AX = mybir.AluOpType, mybir.ActivationFunctionType, mybir.AxisListType

    xs_dram = nc.dram_tensor("xs_sorted", [MT * P, HID], f32, kind="Internal").ap()
    ys_dram = nc.dram_tensor("ys_sorted", [MT * P, HID], f32, kind="Internal").ap()

    ctx = ExitStack()
    with ctx:
        def sem(name):
            return ctx.enter_context(nc.semaphore(name))

        def sb(c, name, shape, dt=f32):
            return c.enter_context(nc.sbuf_tensor(name, shape, dt))

        ident = sb(ctx, "ident", [P, P])
        ones_b = sb(ctx, "ones_b", [P, P], bf16)
        before_b = sb(ctx, "before_b", [P, P], bf16)
        stats = sb(ctx, "stats", [P, NT, 6])
        aggr = sb(ctx, "aggr", [P, NT, 2])
        rstd = sb(ctx, "rstd", [P, NT])
        neg_max = sb(ctx, "neg_max", [P, 2, 4 * GH])
        max_rows = sb(ctx, "max_rows", [4 * GH, 2, P], f32r)
        q_hi = sb(ctx, "q_hi", [P, NT, S], f32r)
        q_lo = sb(ctx, "q_lo", [P, NT, S], f32r)
        k_hi = sb(ctx, "k_hi", [P, NT, S], f32r)
        k_lo = sb(ctx, "k_lo", [P, NT, S], f32r)
        o_all = q_hi[:, :, :].bitcast(f32)
        wo_sb = q_lo[:, 0:HC, :].bitcast(f32)
        gathered = [t[:, :, :].bitcast(f32) for t in (k_hi, k_lo)]

        att = ExitStack()
        qs = [sb(att, f"q_stack{r}", [P, 2, S], f32r) for r in range(RING)]
        ks = [sb(att, f"k_stack{r}", [P, 2, S], f32r) for r in range(RING)]
        v_ones = sb(att, "v_ones", [P, NT, NH, 2 * D])
        o_norm = sb(att, "o_norm", [P, 2, S])
        sums = sb(att, "sums", [P, S])
        pro = ExitStack()
        wq_sb = sb(pro, "wq_sb", [P, HC, HID])
        wk_sb = sb(pro, "wk_sb", [P, HC, HID])
        wv_sb = sb(pro, "wv_sb", [P, HC, HID])
        x_sb = sb(pro, "x_sb", [P, NT, HID])
        xn_sb = sb(pro, "xn_sb", [P, TPB, HID])
        xnT = sb(pro, "xnT", [P, HC, T])
        pro.close()
        probs_t = sb(att, "probs_t", [P, 2, GH, TPB, S])
        att.close()

        x1 = sb(ctx, "x1", [P, NT, HID])
        xn2 = sb(ctx, "xn2", [P, NT, HID])
        xn2T = sb(ctx, "xn2T", [P, 2, HC, P])
        gw_sb = sb(ctx, "gw_sb", [P, HC, E])
        w13_sb = [sb(ctx, f"w13_sb{r}", [P, HC, 2 * F]) for r in range(2)]
        w2_sb = [sb(ctx, f"w2_sb{r}", [P, FC, HID]) for r in range(2)]
        xg = sb(ctx, "xg", [P, 2, HID])
        xgT = sb(ctx, "xgT", [P, HC, P])
        gate = sb(ctx, "gate", [P, F])
        act = sb(ctx, "act", [P, F])
        actT = sb(ctx, "actT", [P, FC, P])
        y_sb = sb(ctx, "y_sb", [P, 2, HID])
        e_of = sb(ctx, "e_of", [P, NT, E])
        e_before = sb(ctx, "e_before", [P, E, E])
        tile_of = sb(ctx, "tile_of", [P, MT, E])
        lmax = sb(ctx, "lmax", [P, NT])
        lsh = sb(ctx, "lsh", [P, NT, E])
        pe_ = sb(ctx, "pe_", [P, NT, E])
        psums = sb(ctx, "psums", [P, NT])
        prec = sb(ctx, "prec", [P, NT])
        pr = sb(ctx, "pr", [P, NT, E])
        top = sb(ctx, "top", [P, NT, E])
        top_i = sb(ctx, "top_i", [P, NT, E], u32)
        top_f = sb(ctx, "top_f", [P, NT, E])
        wsum = sb(ctx, "wsum", [P, NT])
        wrec = sb(ctx, "wrec", [P, NT])
        wtok = sb(ctx, "wtok", [P, TOPK, NT])
        pick = sb(ctx, "pick", [P, TOPK, NT, E])
        picks = sb(ctx, "picks", [P, NT, E], bf16)
        n_i = sb(ctx, "n_i", [P, E], i32)
        c_i = sb(ctx, "c_i", [P, E], i32)
        c_f = sb(ctx, "c_f", [P, E])
        c_bef = sb(ctx, "c_bef", [P, E, E])
        first = sb(ctx, "first", [P, E])
        ends = sb(ctx, "ends", [P, E])
        slot_e = sb(ctx, "slot_e", [P, NT, E])
        slot_p = sb(ctx, "slot_p", [P, TOPK, NT, E])
        slot_f = sb(ctx, "slot_f", [P, TOPK, NT])
        slot_i = sb(ctx, "slot_i", [P, TOPK, NT], u32)
        passed = sb(ctx, "passed", [P, MT, E])
        tile_f = sb(ctx, "tile_f", [P, MT])
        tile_i = sb(ctx, "tile_i", [P, MT], i32)

        ps4 = ctx.enter_context(nc.psum_tensor("ps4", [P, 4, 512], f32))
        ps2 = ctx.enter_context(nc.psum_tensor("ps2", [P, 2, 512], f32))
        ps_o = ctx.enter_context(nc.psum_tensor("ps_o", [P, 512], f32))
        ps_m = ctx.enter_context(nc.psum_tensor("ps_m", [P, 512], f32))
        banks = [ps4[:, i, :] for i in range(4)] + [ps2[:, i, :] for i in range(2)] + [ps_o[:, :], ps_m[:, :]]
        NB = len(banks)

        s_x = [sem(f"s_x{b}") for b in range(B)]
        s_wq, s_wk, s_wv, s_wo, s_gw = (sem(n) for n in ("s_wq", "s_wk", "s_wv", "s_wo", "s_gw"))
        s_const = sem("s_const")
        s_dve = sem("s_dve")
        s_var, s_std = sem("s_var"), sem("s_std")
        s_xn = sem("s_xn")
        s_job = sem("s_job")
        s_ja = sem("s_ja")
        s_jd = sem("s_jd")
        s_stack = [sem(f"s_stack{r}") for r in range(RING)]
        s_row = [sem(f"s_row{r}") for r in range(RING)]
        s_sn = sem("s_sn")
        s_mx = sem("s_mx")
        s_mt = sem("s_mt")
        s_mr = sem("s_mr")
        s_st = sem("s_st")
        s_ex = sem("s_ex")
        s_pv = sem("s_pv")
        s_on = sem("s_on")
        s_oc = [sem(f"s_oc{r}") for r in range(2)]
        s_zero = sem("s_zero")
        s_zt = sem("s_zt")
        s_zs = sem("s_zs")
        s_op, s_res, s_xn2, s_t2, s_t2e, s_lg = (sem(n) for n in ("s_op", "s_res", "s_xn2", "s_t2", "s_t2e", "s_lg"))
        s_lsh, s_lex, s_pick, s_rank, s_slot = (sem(n) for n in ("s_lsh", "s_lex", "s_pick", "s_rank", "s_slot"))
        s_scat = sem("s_scat")
        s_w13 = [sem(f"s_w13_{r}") for r in range(2)]
        s_w2 = [sem(f"s_w2_{r}") for r in range(2)]
        s_xg = [sem(f"s_xg{r}") for r in range(2)]
        s_l1, s_l2, s_xt, s_at = (sem(n) for n in ("s_l1", "s_l2", "s_xt", "s_at"))
        s_xe, s_ae, s_ad, s_silu, s_act, s_ye = (sem(n) for n in ("s_xe", "s_ae", "s_ad", "s_silu", "s_act", "s_ye"))
        s_ys = [sem(f"s_ys{r}") for r in range(2)]
        s_g = [sem(f"s_g{n}") for n in range(2)]
        s_half, s_fin, s_out = sem("s_half"), sem("s_fin"), sem("s_out")

        jobs = []
        for b in range(B):
            jobs += [("t", b, i) for i in range(TPB)]
            jobs += [(kind, b, i) for kind in "qk" for i in range(HC)]
            jobs += [("v", b, i) for i in range(TPB)]
        n_of = {j: n for n, j in enumerate(jobs)}
        a_count = [n + 1 for n in range(len(jobs))]
        d_count, c = [], 0
        for j in jobs:
            c += j[0] in "qk"
            d_count.append(c)

        def job_read(eng, n):
            if jobs[n][0] in "qk":
                eng.wait_ge(s_jd, d_count[n])
            eng.wait_ge(s_ja, a_count[n])

        def head_at(g, j):
            return 64 * (j % 2), j // 2

        def scores_at(u2):
            j, qt = divmod(u2, TPB)
            return j, qt, (j % 2) * 8 + (j // 2) * TPB + qt

        block = ctx.enter_context(nc.Block())

        @block.sync
        def _(sp):
            x_t = x.rearrange("(n p) h -> p n h", p=P)
            sp.dma_start(x_sb[:, 0:TPB, :], x_t[:, 0:TPB, :]).then_inc(s_x[0], 16)
            sp.dma_start(wq_sb[:, :, :], wq.rearrange("p (c e) -> p c e", c=HC)).then_inc(s_wq, 16)
            sp.dma_start(wk_sb[:, :, :], wk.rearrange("p (c e) -> p c e", c=HC)).then_inc(s_wk, 16)
            sp.dma_start(x_sb[:, TPB:NT, :], x_t[:, TPB:NT, :]).then_inc(s_x[1], 16)
            sp.dma_start(wv_sb[:, :, :], wv.rearrange("p (c e) -> p c e", c=HC)).then_inc(s_wv, 16)
            sp.wait_ge(s_const, 5)
            for s in range(-3, NG + 1):
                g = s + 3
                if g < NG:
                    b, r = g // 8, g % RING
                    if s >= 1:
                        sp.wait_ge(s_st, UNITS * s)
                    h0, slot = 64 * (g % 2), g // 2
                    last = jobs[n_of[("k", b, (g // 2) % HC)]]
                    sp.wait_ge(s_jd, d_count[n_of[last]])
                    for par in range(2):
                        for part, (qsrc, ksrc) in enumerate(((q_hi, k_hi), (q_lo, k_hi), (q_hi, k_lo))):
                            for p in range(2):
                                lo = h0 + 32 * par + D * p
                                dst = slice(64 * par + D * part, 64 * par + D * (part + 1))
                                sp.dma_start(qs[r][dst, p, :].bitcast(f32), qsrc[lo:lo + D, slot, :].bitcast(f32)).then_inc(s_stack[r], 16)
                                sp.dma_start(ks[r][dst, p, :].bitcast(f32), ksrc[lo:lo + D, slot, :].bitcast(f32)).then_inc(s_stack[r], 16)
                g = s + 2
                if 0 <= g < NG:
                    r = g % RING
                    sp.wait_ge(s_mr, g + 1)
                    for par in range(2):
                        row = 64 * par + ROWS
                        sp.dma_start(qs[r][row:row + 1, :, :].bitcast(f32).rearrange("a p (t c) -> a (p t) c", c=P),
                                     max_rows[8 * par:8 * par + 8, g % 2, :].bitcast(f32)).then_inc(s_row[r], 16)
                g = s - 1
                if g >= 0:
                    sp.wait_ge(s_on, g + 1)
                    for j in range(GH):
                        lo = 64 * (g % 2) + D * j
                        sp.dma_start(o_all[lo:lo + D, g // 2, :],
                                     o_norm[32 * j:32 * j + D, g % 2, :]).then_inc(s_oc[g % 2], 16)
                if g == 8:
                    sp.dma_start(wo_sb, wo.rearrange("p (c e) -> p c e", c=HC)).then_inc(s_wo, 16)
            sp.wait_ge(s_pv, NG)
            sp.wait_ge(s_on, NG)
            sp.dma_start(x1[:, :, :], x_t).then_inc(s_x[0], 16)
            sp.dma_start(gw_sb[:, :, :], gw.rearrange("p (c e) -> p c e", c=HC)).then_inc(s_gw, 16)

            sp.wait_ge(s_slot, 1)

            def loads(i, r):
                e = sp.value_load(tile_i[0:1, bass.ds(i, 1)], min_val=0, max_val=E - 1)
                sp.dma_start(xg[:, r, :], xs_dram[bass.ds(i * P, P), :]).then_inc(s_xg[r], 16)
                sp.dma_start(w13_sb[r][:, :, :].rearrange("p c f -> p (c f)"),
                             w13[bass.ds(e, 1), :, :].rearrange("a p n -> (a p) n")).then_inc(s_w13[r], 16)
                return e

            def loads2(e, r):
                sp.dma_start(w2_sb[r][:, 0:FC - 1, :].rearrange("p c f -> p (c f)"),
                             w2[bass.ds(e, 1), :, :].rearrange("a p n -> (a p) n")).then_inc(s_w2[r], 16)
                sp.dma_start(w2_sb[r][0:FTAIL, FC - 1, :],
                             w2t[bass.ds(e, 1), :, :].rearrange("a p n -> (a p) n")).then_inc(s_w2[r], 16)

            def store(i, r):
                sp.wait_ge(s_ye, i + 1)
                sp.dma_start(ys_dram[bass.ds(i * P, P), :], y_sb[:, r, :]).then_inc(s_ys[r], 16)

            sp.wait_ge(s_scat, 16 * NT * TOPK)
            for i in range(2):
                loads2(loads(i, i), i)

            def step(i, r):
                sp.wait_ge(s_l1, i + 1)
                e = loads(i + 2, r)
                sp.wait_ge(s_l2, i + 1)
                loads2(e, r)
                store(i, r)

            with sp.Fori(0, (MT - 3) // 2) as m:
                step(2 * m, 0)
                step(2 * m + 1, 1)
            i = MT - 3
            step(i, i % 2)
            for i in (MT - 2, MT - 1):
                store(i, i % 2)
            for t in range(NT):
                sp.wait_ge(s_fin, t + 1)
                sp.dma_start(out[t * P:(t + 1) * P, :], x1[:, t, :]).then_inc(s_out, 16)
            sp.wait_ge(s_out, 16 * NT)

        @block.gpsimd
        def _(pool):
            pool.memset(ident[:, :], 0.0).then_inc(s_zero, 1)
            pool.memset(before_b[:, :], 1.0).then_inc(s_zero, 1)
            pool.wait_ge(s_zero, 2)
            pool.affine_select(out=ident[:, :], in_=ident[:, :], compare_op=ALU.not_equal, fill=1.0,
                               base=0, pattern=[[-1, P]], channel_multiplier=1).then_inc(s_const, 1)
            pool.affine_select(out=before_b[:, :], in_=before_b[:, :], compare_op=ALU.is_gt, fill=0.0,
                               base=0, pattern=[[1, P]], channel_multiplier=-1).then_inc(s_const, 1)
            pool.memset(ones_b[:, :], 1.0).then_inc(s_const, 1)
            pool.memset(v_ones[:, :, :, D:2 * D], 1.0).then_inc(s_const, 1)
            for r in range(RING):
                last = pool.memset(ks[r][:, :, :].bitcast(f32), 1.0)
            last.then_inc(s_const, 1)
            pool.wait_ge(s_pv, NG)
            pool.wait_ge(s_on, NG)
            pool.memset(w13_sb[0][:, :, :], 0.0).then_inc(s_zt, 1)
            pool.iota(e_of[:, :, :], pattern=[[0, NT], [1, E]], base=0, channel_multiplier=0,
                      allow_small_or_imprecise_dtypes=True).then_inc(s_const, 1)
            pool.iota(tile_of[:, :, :], pattern=[[1, MT], [0, E]], base=0, channel_multiplier=0,
                      allow_small_or_imprecise_dtypes=True).then_inc(s_const, 1)
            pool.memset(e_before[:, :, :], 1.0).then_inc(s_zt, 1)
            pool.wait_ge(s_zt, 2)
            pool.affine_select(out=e_before[:, :, :], in_=e_before[:, :, :], compare_op=ALU.is_gt, fill=0.0,
                               base=0, pattern=[[1, E], [-1, E]], channel_multiplier=0).then_inc(s_const, 1)
            xs_t = xs_dram.rearrange("(n p) h -> p n h", p=P)
            zeros = w13_sb[0][:, :, :].rearrange("p c f -> p (c f)")
            n0 = 0
            while n0 < MT:
                n = min(12, MT - n0)
                pool.dma_start(xs_t[:, n0:n0 + n, :],
                               zeros[:, 0:n * HID].rearrange("p (n h) -> p n h", n=n)).then_inc(s_zs, 16)
                n0 += n
            pool.wait_ge(s_zs, 16 * 2)
            pool.wait_ge(s_slot, 1)
            for t in range(NT):
                for k in range(TOPK):
                    pool.indirect_dma_start(
                        out=xs_dram[:, :], out_offset=bass.IndirectOffsetOnAxis(ap=slot_i[:, k, t:t + 1], axis=0),
                        in_=xn2[:, t, :], in_offset=None).then_inc(s_scat, 16)
            for r in range(2):
                pool.wait_ge(s_ys[r], 16 * ((MT + 1 - r) // 2))
            for t in range(NT):
                for k in range(TOPK):
                    pool.indirect_dma_start(
                        out=gathered[k][:, t, :], out_offset=None, in_=ys_dram[:, :],
                        in_offset=bass.IndirectOffsetOnAxis(ap=slot_i[:, k, t:t + 1], axis=0)).then_inc(s_g[k], 16)

        @block.tensor
        def _(pe):
            pe.wait_ge(s_const, 5)
            for n, (kind, b, i) in enumerate(jobs):
                if n >= NB:
                    job_read(pe, n - NB)
                o = banks[n % NB]
                if kind == "t":
                    pe.wait_ge(s_xn, b * TPB + i + 1)
                    for c in range(HC):
                        last = pe.transpose(o[:, c * P:(c + 1) * P], xn_sb[:, i, c * P:(c + 1) * P], ident[:, :])
                elif kind in "qk":
                    w = wq_sb if kind == "q" else wk_sb
                    pe.wait_ge(s_wq if kind == "q" else s_wk, 16)
                    pe.wait_ge(s_ja, a_count[n_of[("t", b, TPB - 1)]])
                    for c in range(HC):
                        last = pe.matmul(o, w[:, c, i * P:(i + 1) * P], xnT[:, c, b * S:(b + 1) * S],
                                         start=(c == 0), stop=(c == HC - 1))
                else:
                    pe.wait_ge(s_wv, 16)
                    t0 = b * S + i * P
                    for c in range(HC):
                        last = pe.matmul(o, xnT[:, c, t0:t0 + P], wv_sb[:, c, :],
                                         start=(c == 0), stop=(c == HC - 1))
                last.then_inc(s_job, 1)
            for n in range(len(jobs) - NB, len(jobs)):
                job_read(pe, n)

            def pv(g, half):
                if half == 0 and g >= 1:
                    pe.wait_ge(s_on, g)
                for kc in (2 * half, 2 * half + 1):
                    for j in range(GH):
                        last = pe.matmul(ps_o[32 * j:32 * j + 32, :],
                                         v_ones[:, (g // 8) * TPB + kc, (g % 8) * GH + j, :],
                                         probs_t[:, g % 2, j, kc, :], start=(kc == 0), stop=(kc == TPB - 1),
                                         tile_position=(0, 32 * j))
                if half:
                    last.then_inc(s_pv, 1)

            for s in range(-2, NG + 1):
                ga = s + 2
                if ga < NG:
                    pe.wait_ge(s_stack[ga % RING], 16 * 24 * (ga // RING + 1))
                if 0 <= s < NG:
                    pe.wait_ge(s_row[s % RING], 32 * (s // RING + 1))
                if s >= 1:
                    pe.wait_ge(s_ex, UNITS * s)
                for u in range(UNITS):
                    if 0 <= s < NG:
                        n = s * UNITS + u
                        if n >= 2:
                            pe.wait_ge(s_ex, n - 1)
                        j, kc2 = divmod(u, 2)
                        base, p = head_at(s, j)
                        for c in range(2):
                            kc = 2 * kc2 + c
                            last = pe.matmul(ps4[:, 2 * (n % 2) + c, :],
                                             ks[s % RING][base:base + ROWS + 1, p, kc * P:(kc + 1) * P],
                                             qs[s % RING][base:base + ROWS + 1, p, :], start=True, stop=True)
                        last.then_inc(s_st, 1)
                    if ga < NG:
                        for c in range(2):
                            j, qt, _ = scores_at(2 * u + c)
                            n = ga * 16 + 2 * u + c
                            base, p = head_at(ga, j)
                            if n >= 2:
                                pe.wait_ge(s_mx, n - 1)
                            pe.matmul(ps2[:, n % 2, :], qs[ga % RING][base:base + ROWS, p, qt * P:(qt + 1) * P],
                                      ks[ga % RING][base:base + ROWS, p, :], start=True, stop=True).then_inc(s_sn, 1)
                    if s >= 1 and u in (3, 7):
                        pv(s - 1, u // 4)
                if ga < NG:
                    pe.wait_ge(s_mx, 16 * (ga + 1))
                    if ga >= 1:
                        pe.wait_ge(s_mr, ga)
                    pe.transpose(ps_m[0:4 * GH, 0:P], neg_max[:, ga % 2, :], ident[:, :]).then_inc(s_mt, 1)

            pe.wait_ge(s_wo, 16)
            for r in range(2):
                pe.wait_ge(s_oc[r], 16 * GH * NG // 2)
            for t in range(NT):
                if t >= 4:
                    pe.wait_ge(s_res, t - 3)
                b, qt = divmod(t, TPB)
                for c in range(HC):
                    last = pe.matmul(ps4[:, t % 4, :], o_all[:, b * HC + c, qt * P:(qt + 1) * P], wo_sb[:, c, :],
                                     start=(c == 0), stop=(c == HC - 1))
                last.then_inc(s_op, 1)
            pe.wait_ge(s_gw, 16)
            for t in range(NT):
                pe.wait_ge(s_xn2, t + 1)
                if t >= 2:
                    pe.wait_ge(s_t2e, t - 1)
                for c in range(HC):
                    last = pe.transpose(ps2[:, t % 2, c * P:(c + 1) * P], xn2[:, t, c * P:(c + 1) * P], ident[:, :])
                last.then_inc(s_t2, 1)
                pe.wait_ge(s_t2e, t + 1)
                for c in range(HC):
                    last = pe.matmul(ps_o[:, t * E:(t + 1) * E], xn2T[:, t % 2, c, :], gw_sb[:, c, :],
                                     start=(c == 0), stop=(c == HC - 1))
                last.then_inc(s_lg, 1)
            pe.wait_ge(s_pick, 1)
            pk = picks[:, :, :].rearrange("p t e -> p (t e)")
            for d in range(1, NT):
                pe.matmul(ps_m[:, d * E:NT * E], ones_b[:, :], pk[:, 0:(NT - d) * E],
                          start=(d == 1), stop=False, skip_group_check=True)
            pe.matmul(ps_m[:, 0:NT * E], before_b[:, :], pk, start=False, stop=True, skip_group_check=True)
            for t in range(NT):
                last = pe.matmul(ps2[:, 0, 0:E], ones_b[:, :], pk[:, t * E:(t + 1) * E],
                                 start=(t == 0), stop=(t == NT - 1))
            last.then_inc(s_rank, 1)

            def rows_in(i, r, n):
                pe.wait_ge(s_xg[r], 16 * n)
                if not (isinstance(i, int) and i == 0):
                    pe.wait_ge(s_xe, i)
                for c in range(HC):
                    last = pe.transpose(ps_m[:, c * P:(c + 1) * P], xg[:, r, c * P:(c + 1) * P], ident[:, :])
                last.then_inc(s_xt, 1)

            def up(i, r, n):
                pe.wait_ge(s_w13[r], 16 * n)
                pe.wait_ge(s_xe, i + 1)
                if not (isinstance(i, int) and i == 0):
                    pe.wait_ge(s_act, i)
                for q in range(4):
                    for c in range(HC):
                        last = pe.matmul(ps4[:, q, 0:FH], xgT[:, c, :], w13_sb[r][:, c, q * FH:(q + 1) * FH],
                                         start=(c == 0), stop=(c == HC - 1))
                return last

            def down(i, r, n):
                pe.wait_ge(s_w2[r], 32 * n)
                pe.wait_ge(s_ae, i + 1)
                pe.wait_ge(s_ad, i + 1)
                if not (isinstance(i, int) and i == 0):
                    pe.wait_ge(s_ye, i)
                for c in range(FC):
                    k = P if c < FC - 1 else FTAIL
                    last = pe.matmul(ps_o[:, :], actT[0:k, c, :], w2_sb[r][0:k, c, :],
                                     start=(c == 0), stop=(c == FC - 1))
                last.then_inc(s_l2, 1)

            def inner_t(i):
                pe.wait_ge(s_act, i + 1)
                for c in range(FC):
                    k = P if c < FC - 1 else FTAIL
                    last = pe.transpose(ps2[0:k, c // 4, (c % 4) * P:(c % 4 + 1) * P],
                                        act[:, c * P:c * P + k], ident[:, :])
                last.then_inc(s_at, 1)

            def step(i, r, n, first=False, more=True):
                up(i, r, n).then_inc(s_l1, 1)
                if more:
                    rows_in(i + 1, 1 - r, n + r)
                if not first:
                    down(i - 1, 1 - r, n - 1 + r)
                inner_t(i)

            rows_in(0, 0, 1)
            step(0, 0, 1, first=True)
            with pe.Fori(0, (MT - 3) // 2) as m:
                step(2 * m + 1, 1, m + 1)
                step(2 * m + 2, 0, m + 2)
            step(MT - 2, (MT - 2) % 2, (MT - 2) // 2 + 1)
            step(MT - 1, (MT - 1) % 2, (MT - 1) // 2 + 1, more=False)
            down(MT - 1, (MT - 1) % 2, (MT - 1) // 2 + 1)

        @block.scalar
        def _(a):
            def root(n, t0):
                a.wait_ge(s_var, n)
                a.activation(rstd[:, t0:t0 + TPB], rstd[:, t0:t0 + TPB], ACT.Sqrt).then_inc(s_std, 1)

            for b in range(B):
                root(b + 1, b * TPB)
            for n, (kind, b, i) in enumerate(jobs):
                o = banks[n % NB]
                a.wait_ge(s_job, n + 1)
                if kind == "t":
                    t0 = b * S + i * P
                    a.activation(xnT[:, :, t0:t0 + P], o.rearrange("p (c t) -> p c t", c=HC), ACT.Copy).then_inc(s_ja, 1)
                elif kind == "v":
                    a.activation(v_ones[:, b * TPB + i, :, 0:D], o.rearrange("p (h d) -> p h d", d=D),
                                 ACT.Copy).then_inc(s_ja, 1)
                else:
                    hi = q_hi if kind == "q" else k_hi
                    a.activation(hi[:, b * HC + i, :], o, ACT.Copy).then_inc(s_ja, 1)
            for s in range(-2, NG + 1):
                if 0 <= s < NG:
                    if s >= 2:
                        a.wait_ge(s_pv, s - 1)
                    for u in range(UNITS):
                        n = s * UNITS + u
                        a.wait_ge(s_st, n + 1)
                        j, kc2 = divmod(u, 2)
                        a.activation(probs_t[:, s % 2, j, 2 * kc2:2 * kc2 + 2, :],
                                     ps4[:, 2 * (n % 2):2 * (n % 2) + 2, :], ACT.Exp, scale=D ** -0.5).then_inc(s_ex, 1)
                ga = s + 2
                if ga < NG:
                    a.wait_ge(s_mt, ga + 1)
                    if ga >= 2:
                        a.wait_ge(s_row[(ga - 2) % RING], 32 * ((ga - 2) // RING + 1))
                    a.activation(max_rows[:, ga % 2, :], ps_m[0:4 * GH, 0:P], ACT.Copy).then_inc(s_mr, 1)
            for t in range(NT):
                if t % TPB == 0:
                    root(B + t // TPB + 1, t)
                a.wait_ge(s_t2, t + 1)
                if t >= 2:
                    a.wait_ge(s_lg, t - 1)
                a.activation(xn2T[:, t % 2, :, :], ps2[:, t % 2, :].rearrange("p (c t) -> p c t", c=HC),
                             ACT.Copy).then_inc(s_t2e, 1)
            a.wait_ge(s_lsh, 1)
            a.activation(pe_[:, :, :], lsh[:, :, :], ACT.Exp).then_inc(s_lex, 1)

            def silu(i):
                a.wait_ge(s_l1, i + 1)
                if not (isinstance(i, int) and i == 0):
                    a.wait_ge(s_act, i)
                a.activation(gate[:, :].rearrange("p (h f) -> p h f", h=2), ps4[:, 0:2, 0:FH],
                             ACT.Silu).then_inc(s_silu, 1)

            def y_out(i, r, turn):
                a.wait_ge(s_l2, i + 1)
                if turn is not None:
                    a.wait_ge(s_ys[r], 16 * turn)
                a.activation(y_sb[:, r, :], ps_o[:, :], ACT.Copy).then_inc(s_ye, 1)

            def inner_out(i):
                a.wait_ge(s_at, i + 1)
                a.activation(actT[:, 0:4, :], ps2[:, 0, :].rearrange("p (c t) -> p c t", c=4), ACT.Copy).then_inc(s_ae, 1)

            silu(0)
            inner_out(0)
            silu(1)
            y_out(0, 0, None)
            inner_out(1)
            silu(2)
            y_out(1, 1, None)
            inner_out(2)
            with a.Fori(0, (MT - 3) // 2) as m:
                silu(2 * m + 3)
                y_out(2 * m + 2, 0, m + 1)
                inner_out(2 * m + 3)
                silu(2 * m + 4)
                y_out(2 * m + 3, 1, m + 1)
                inner_out(2 * m + 4)
            y_out(MT - 1, 0, (MT - 1) // 2)

        @block.vector
        def _(v):
            chain, norms = [0], [0]

            def link(ins):
                chain[0] += 1
                ins.then_inc(s_dve, 1)
                v.wait_ge(s_dve, chain[0])

            def norm(src, dst, t0, n, done, free):
                for t in range(t0, t0 + n):
                    ins = v.bn_stats(stats[:, t, :], src[:, t, :])
                link(ins)
                for t in range(t0, t0 + n):
                    ins = v.bn_aggr(aggr[:, t, :], stats[:, t, :])
                link(ins)
                v.tensor_scalar(rstd[:, t0:t0 + n], aggr[:, t0:t0 + n, 1], EPS, None, ALU.add).then_inc(s_var, 1)
                norms[0] += 1
                v.wait_ge(s_std, norms[0])
                link(v.reciprocal(rstd[:, t0:t0 + n], rstd[:, t0:t0 + n]))
                if free is not None:
                    v.wait_ge(s_job, free)
                for k in range(n):
                    t = t0 + k
                    v.tensor_scalar(dst(t), src[:, t, :], aggr[:, t, 0:1], rstd[:, t:t + 1],
                                    ALU.subtract, ALU.mult).then_inc(done, 1)

            for b in range(B):
                v.wait_ge(s_x[b], 16)
                norm(x_sb, lambda t: xn_sb[:, t % TPB, :], b * TPB, TPB, s_xn, n_of[("t", 0, TPB - 1)] + 1 if b else None)
            for n, (kind, b, i) in enumerate(jobs):
                if kind in "qk":
                    hi, lo = (q_hi, q_lo) if kind == "q" else (k_hi, k_lo)
                    v.wait_ge(s_ja, a_count[n])
                    v.tensor_tensor(lo[:, b * HC + i, :], banks[n % NB], hi[:, b * HC + i, :].bitcast(f32),
                                    ALU.subtract).then_inc(s_jd, 1)
            for s in range(-2, NG + 1):
                ga = s + 2
                if ga < NG:
                    if ga >= 2:
                        v.wait_ge(s_mt, ga - 1)
                    for u2 in range(16):
                        _, _, col = scores_at(u2)
                        n = ga * 16 + u2
                        v.wait_ge(s_sn, n + 1)
                        v.tensor_reduce(neg_max[:, ga % 2, col:col + 1], ps2[:, n % 2, :], AX.X, ALU.max,
                                        negate=True).then_inc(s_mx, 1)
                g = s - 1
                if g >= 0:
                    v.wait_ge(s_pv, g + 1)
                    if g >= 2:
                        v.wait_ge(s_oc[g % 2], 16 * GH * (g // 2))
                    link(v.stream_shuffle(sums[:, :], ps_o[:, :], [D] * 32))
                    link(v.reciprocal(sums[:, :], sums[:, :]))
                    v.tensor_tensor(o_norm[:, g % 2, :], ps_o[:, :], sums[:, :], ALU.mult).then_inc(s_on, 1)
            v.wait_ge(s_x[0], 32)
            for t in range(NT):
                v.wait_ge(s_op, t + 1)
                ins = v.tensor_tensor(x1[:, t, :], ps4[:, t % 4, :], x1[:, t, :], ALU.add).then_inc(s_res, 1)
                if t % TPB == TPB - 1:
                    v.wait_ge(s_res, t + 1)
                    norm(x1, lambda t: xn2[:, t, :], t + 1 - TPB, TPB, s_xn2, None)
            v.wait_ge(s_lg, NT)
            v.wait_ge(s_const, 8)
            lg = ps_o[:, 0:NT * E].rearrange("p (t e) -> p t e", e=E)
            wide = lambda a: a.unsqueeze(2).broadcast_to([P, NT, E])
            link(v.tensor_reduce(lmax[:, :], lg, AX.X, ALU.max))
            v.tensor_tensor(lsh[:, :, :], lg, wide(lmax[:, :]), ALU.subtract).then_inc(s_lsh, 1)
            v.wait_ge(s_lex, 1)
            link(v.tensor_reduce(psums[:, :], pe_[:, :, :], AX.X, ALU.add))
            link(v.reciprocal(prec[:, :], psums[:, :]))
            link(v.tensor_tensor(pr[:, :, :], pe_[:, :, :], wide(prec[:, :]), ALU.mult))
            for t in range(NT):
                ins = v.max(top[:, t, :], pr[:, t, :])
            link(ins)
            for t in range(NT):
                ins = v.max_index(top_i[:, t, :], top[:, t, :], pr[:, t, :])
            link(ins)
            v.tensor_reduce(wsum[:, :], top[:, :, 0:TOPK], AX.X, ALU.add)
            link(v.tensor_copy(top_f[:, :, :], top_i[:, :, :]))
            v.reciprocal(wrec[:, :], wsum[:, :])
            for k in range(TOPK):
                ins = v.tensor_tensor(pick[:, k, :, :], e_of[:, :, :], wide(top_f[:, :, k]), ALU.is_equal)
            link(ins)
            v.tensor_tensor(picks[:, :, :], pick[:, 0, :, :], pick[:, 1, :, :], ALU.add).then_inc(s_pick, 1)
            for k in range(TOPK):
                v.tensor_tensor(wtok[:, k, :], top[:, :, k], wrec[:, :], ALU.mult)
            v.wait_ge(s_rank, 1)
            link(v.tensor_scalar(n_i[:, :], ps2[:, 0, 0:E], float(P - 1), None, ALU.add))
            link(v.tensor_scalar(c_i[:, :], n_i[:, :], 7, None, ALU.arith_shift_right))
            link(v.tensor_copy(c_f[:, :], c_i[:, :]))
            link(v.tensor_tensor(c_bef[:, :, :], e_before[:, :, :],
                                 c_f[:, :].unsqueeze(1).broadcast_to([P, E, E]), ALU.mult))
            link(v.tensor_reduce(first[:, :], c_bef[:, :, :], AX.X, ALU.add))
            v.scalar_tensor_tensor(slot_e[:, :, :], first[:, :].unsqueeze(1).broadcast_to([P, NT, E]), float(P),
                                   ps_m[:, 0:NT * E].rearrange("p (t e) -> p t e", e=E), ALU.mult, ALU.add)
            link(v.tensor_tensor(ends[:, :], first[:, :], c_f[:, :], ALU.add))
            for k in range(TOPK):
                v.tensor_tensor(slot_p[:, k, :, :], pick[:, k, :, :], slot_e[:, :, :], ALU.mult)
            link(v.tensor_tensor(passed[:, :, :], ends[:, :].unsqueeze(1).broadcast_to([P, MT, E]),
                                 tile_of[:, :, :], ALU.is_le))
            v.tensor_reduce(slot_f[:, :, :], slot_p[:, :, :, :], AX.X, ALU.add)
            link(v.tensor_reduce(tile_f[:, :], passed[:, :, :], AX.X, ALU.add))
            v.tensor_copy(slot_i[:, :, :], slot_f[:, :, :])
            v.tensor_scalar(tile_i[:, :], tile_f[:, :], float(E - 1), None, ALU.min).then_inc(s_slot, 1)

            def rows_t(i):
                v.wait_ge(s_xt, i + 1)
                v.tensor_copy(xgT[:, :, :].rearrange("p c t -> p (c t)"), ps_m[:, :]).then_inc(s_xe, 1)

            def gated(i):
                v.wait_ge(s_silu, i + 1)
                if not (isinstance(i, int) and i == 0):
                    v.wait_ge(s_at, i)
                v.tensor_tensor(act[:, :].rearrange("p (h f) -> p h f", h=2), gate[:, :].rearrange("p (h f) -> p h f", h=2),
                                ps4[:, 2:4, 0:FH], ALU.mult).then_inc(s_act, 1)

            def inner_out(i):
                v.wait_ge(s_at, i + 1)
                v.tensor_copy(actT[:, 4:6, :].rearrange("p c t -> p (c t)"), ps2[:, 1, 0:2 * P])
                v.tensor_copy(actT[0:FTAIL, FC - 1, :], ps2[0:FTAIL, 1, 2 * P:3 * P]).then_inc(s_ad, 1)

            rows_t(0)
            gated(0)
            rows_t(1)
            inner_out(0)
            with v.Fori(1, MT - 1) as i:
                gated(i)
                rows_t(i + 1)
                inner_out(i)
            gated(MT - 1)
            inner_out(MT - 1)
            v.wait_ge(s_g[0], 16 * NT)
            v.wait_ge(s_g[1], 16 * NT)
            for t in range(NT):
                v.scalar_tensor_tensor(x1[:, t, :], gathered[0][:, t, :], wtok[:, 0, t:t + 1], x1[:, t, :],
                                       ALU.mult, ALU.add).then_inc(s_half, 1)
                v.wait_ge(s_half, t + 1)
                v.scalar_tensor_tensor(x1[:, t, :], gathered[1][:, t, :], wtok[:, 1, t:t + 1], x1[:, t, :],
                                       ALU.mult, ALU.add).then_inc(s_fin, 1)


def kernel(L0_attn_x, L0_attn_w_q, L0_attn_w_k, L0_attn_w_v, L0_attn_w_o,
           L0_ffn_gate_w, L0_ffn_w1, L0_ffn_w2, L0_ffn_w3):
    import numpy as np
    import concourse.bacc as bacc
    from concourse.bass_utils import run_bass_kernel_spmd

    def rows_first(w_t):
        r, n = w_t.shape
        return np.ascontiguousarray(w_t.reshape(r // P, P, n).transpose(1, 0, 2).reshape(P, -1))

    order = np.array([(4 * g + 2 * p + par) * D + d
                      for g in range(NH // GH) for par in range(2) for p in range(2) for d in range(D)])
    w1, w2, w3 = (np.asarray(w) for w in (L0_ffn_w1, L0_ffn_w2, L0_ffn_w3))
    w13 = np.concatenate([w1, w3], axis=1).transpose(0, 2, 1)
    w13 = np.ascontiguousarray(w13.reshape(E, HC, P, 2 * F).transpose(0, 2, 1, 3).reshape(E, P, -1))
    w2_t = w2.transpose(0, 2, 1)
    main = (FC - 1) * P
    w2_main = np.ascontiguousarray(
        w2_t[:, :main, :].reshape(E, FC - 1, P, HID).transpose(0, 2, 1, 3).reshape(E, P, -1))
    arrays = {
        "x": np.asarray(L0_attn_x).reshape(T, HID),
        "wq": rows_first(np.asarray(L0_attn_w_q).T[:, order]),
        "wk": rows_first(np.asarray(L0_attn_w_k).T[:, order]),
        "wv": rows_first(np.asarray(L0_attn_w_v).T),
        "wo": rows_first(np.asarray(L0_attn_w_o).T),
        "gw": rows_first(np.asarray(L0_ffn_gate_w).T),
        "w13": w13,
        "w2": w2_main,
        "w2t": np.ascontiguousarray(w2_t[:, main:, :]),
    }
    nc = bacc.Bacc("TRN2", target_bir_lowering=False, num_devices=1)
    args = [nc.dram_tensor(k, a.shape, mybir.dt.from_np(a.dtype), kind="ExternalInput").ap() for k, a in arrays.items()]
    args.append(nc.dram_tensor("out", (T, HID), mybir.dt.float32, kind="ExternalOutput").ap())
    moe_layer(nc, *args)
    r = run_bass_kernel_spmd(nc, [arrays], core_ids=[0])
    return r.results[0]["out"].reshape(B, S, HID)
```

```python
import concourse.bass as bass
from concourse import mybir
from contextlib import ExitStack

P = 128
B, S, HID = 2, 512, 512
NH, D = 32, 16
T = B * S
NT = T // P
TPB = S // P
HC = HID // P
E, F, TOPK = 8, 800, 2
FH = F // 2
FC = -(-F // P)
FTAIL = F - (FC - 1) * P
GH = 4
NG = B * NH // GH
UNITS = 8
PROD = 3
ROWS = PROD * D
MROW = 64 + ROWS
RING = 3
MT = (T * TOPK - E) // P + E
EPS = 1e-5


def moe_layer(nc: bass.Bass, x, wq, wk, wv, wo, gw, w13, w2, w2t, out):
    f32, f32r, bf16 = mybir.dt.float32, mybir.dt.float32r, mybir.dt.bfloat16
    i32, u32 = mybir.dt.int32, mybir.dt.uint32
    ALU, ACT, AX = mybir.AluOpType, mybir.ActivationFunctionType, mybir.AxisListType

    xs_dram = nc.dram_tensor("xs_sorted", [MT * P, HID], f32, kind="Internal").ap()
    ys_dram = nc.dram_tensor("ys_sorted", [MT * P, HID], f32, kind="Internal").ap()

    ctx = ExitStack()
    with ctx:
        def sem(name):
            return ctx.enter_context(nc.semaphore(name))

        def sb(c, name, shape, dt=f32):
            return c.enter_context(nc.sbuf_tensor(name, shape, dt))

        ident = sb(ctx, "ident", [P, P])
        ones_b = sb(ctx, "ones_b", [P, P], bf16)
        before_b = sb(ctx, "before_b", [P, P], bf16)
        stats = sb(ctx, "stats", [P, NT, 6])
        aggr = sb(ctx, "aggr", [P, NT, 2])
        rstd = sb(ctx, "rstd", [P, NT])
        neg_max = sb(ctx, "neg_max", [P, 2, 4 * GH])
        max_rows = sb(ctx, "max_rows", [4 * GH, 2, P], f32r)
        e_of = sb(ctx, "e_of", [P, NT, E])
        e_before = sb(ctx, "e_before", [P, E, E])
        tile_of = sb(ctx, "tile_of", [P, MT, E])
        gw_sb = sb(ctx, "gw_sb", [P, HC, E])

        proj = ExitStack()
        q_hi = sb(proj, "q_hi", [P, NT, S], f32r)
        q_lo = sb(proj, "q_lo", [P, NT, S], f32r)
        k_hi = sb(proj, "k_hi", [P, NT, S], f32r)
        k_lo = sb(proj, "k_lo", [P, NT, S], f32r)
        o_all = q_hi[:, :, :].bitcast(f32)
        wo_sb = q_lo[:, 0:HC, :].bitcast(f32)
        gathered = [t[:, :, :].bitcast(f32) for t in (k_hi, k_lo)]
        att = ExitStack()
        q_shape, k_shape = [P, 2, 4, S], [P, 4, S]
        q0 = sb(att, "q_stack0", q_shape, f32r)
        k0 = sb(att, "k_stack0", k_shape, f32r)
        k1 = sb(att, "k_stack1", k_shape, f32r)
        v_ones = sb(att, "v_ones", [P, NT, NH, D, 2])
        sum_rec = sb(att, "sum_rec", [P, 2, GH * S // P])
        rec_row = sb(att, "rec_row", [P, S])
        pro = ExitStack()
        x_sb = sb(pro, "x_sb", [P, NT, HID])
        xn_sb = sb(pro, "xn_sb", [P, TPB, HID])
        xnT = sb(pro, "xnT", [P, HC, T])
        wq_sb = sb(pro, "wq_sb", [P, HC, HID])
        wk_sb = sb(pro, "wk_sb", [P, HC, HID])
        wv_sb = sb(pro, "wv_sb", [P, HC, HID])
        pro.close()
        q1 = sb(att, "q_stack1", q_shape, f32r)
        q2 = sb(att, "q_stack2", q_shape, f32r)
        k2 = sb(att, "k_stack2", k_shape, f32r)
        qs, ks = (q0, q1, q2), (k0, k1, k2)
        probs_t = sb(att, "probs_t", [P, 2, GH, S])
        o_raw = sb(att, "o_raw", [P, 2, S])
        rec_all = sb(att, "rec_all", [P, S])
        o_norm = sb(att, "o_norm", [P, 2, S])
        att.close()
        proj.close()

        w13_hi = sb(ctx, "w13_hi", [P, 4, HC, FH], f32r)
        w13_lo = sb(ctx, "w13_lo", [P, 4, HC, FH], f32r)
        w2_hi = sb(ctx, "w2_hi", [P, FC, HID], f32r)
        x1 = sb(ctx, "x1", [P, NT, HID])
        xn2 = sb(ctx, "xn2", [P, NT, HID])
        xn2T = k_lo[:, 0:2, :].bitcast(f32).rearrange("p a (c t) -> p a c t", c=HC)
        w13_sb = sb(ctx, "w13_sb", [P, 4, HC, FH])
        w2_sb = sb(ctx, "w2_sb", [P, FC, HID])
        w2_lo = sb(ctx, "w2_lo", [P, FC, HID], f32r)
        xg = sb(ctx, "xg", [P, HID])
        xgT_hi = sb(ctx, "xgT_hi", [P, HC, P], f32r)
        xgT_lo = sb(ctx, "xgT_lo", [P, HC, P], f32r)
        gate = sb(ctx, "gate", [P, F])
        act = sb(ctx, "act", [P, F])
        actT_hi = sb(ctx, "actT_hi", [P, FC, P], f32r)
        actT_lo = sb(ctx, "actT_lo", [P, FC, P], f32r)
        y_sb = sb(ctx, "y_sb", [P, HID])
        lmax = sb(ctx, "lmax", [P, NT])
        lsh = sb(ctx, "lsh", [P, NT, E])
        pe_ = sb(ctx, "pe_", [P, NT, E])
        psums = sb(ctx, "psums", [P, NT])
        prec = sb(ctx, "prec", [P, NT])
        pr = sb(ctx, "pr", [P, NT, E])
        top = sb(ctx, "top", [P, NT, E])
        top_i = sb(ctx, "top_i", [P, NT, E], u32)
        top_f = sb(ctx, "top_f", [P, NT, E])
        wsum = sb(ctx, "wsum", [P, NT])
        wrec = sb(ctx, "wrec", [P, NT])
        wtok = sb(ctx, "wtok", [P, TOPK, NT])
        pick = sb(ctx, "pick", [P, TOPK, NT, E])
        picks = sb(ctx, "picks", [P, NT, E], bf16)
        n_i = sb(ctx, "n_i", [P, E], i32)
        c_i = sb(ctx, "c_i", [P, E], i32)
        c_f = sb(ctx, "c_f", [P, E])
        c_bef = sb(ctx, "c_bef", [P, E, E])
        first = sb(ctx, "first", [P, E])
        ends = sb(ctx, "ends", [P, E])
        slot_e = sb(ctx, "slot_e", [P, NT, E])
        slot_p = sb(ctx, "slot_p", [P, TOPK, NT, E])
        slot_f = sb(ctx, "slot_f", [P, TOPK, NT])
        slot_i = sb(ctx, "slot_i", [P, TOPK, NT], u32)
        passed = sb(ctx, "passed", [P, MT, E])
        tile_f = sb(ctx, "tile_f", [P, MT])
        tile_i = sb(ctx, "tile_i", [P, MT], i32)
        new_f = sb(ctx, "new_f", [P, MT])
        new_i = sb(ctx, "new_i", [P, MT], i32)

        ps4 = ctx.enter_context(nc.psum_tensor("ps4", [P, 4, 512], f32))
        ps2 = ctx.enter_context(nc.psum_tensor("ps2", [P, 2, 512], f32))
        ps_o = ctx.enter_context(nc.psum_tensor("ps_o", [P, 512], f32))
        ps_m = ctx.enter_context(nc.psum_tensor("ps_m", [P, 512], f32))
        banks = [ps4[:, i, :] for i in range(4)] + [ps2[:, i, :] for i in range(2)] + [ps_o[:, :], ps_m[:, :]]
        NB = len(banks)

        s_x = [sem(f"s_x{b}") for b in range(B)]
        s_wq, s_wk, s_wv, s_wo, s_gw = (sem(n) for n in ("s_wq", "s_wk", "s_wv", "s_wo", "s_gw"))
        s_const = sem("s_const")
        s_dve = sem("s_dve")
        s_var, s_std = sem("s_var"), sem("s_std")
        s_xn = sem("s_xn")
        s_job = sem("s_job")
        s_ja = sem("s_ja")
        s_jd = sem("s_jd")
        s_stack = [sem(f"s_stack{r}") for r in range(RING)]
        s_row = [sem(f"s_row{r}") for r in range(4)]
        s_ones = sem("s_ones")
        s_sn = sem("s_sn")
        s_mx = sem("s_mx")
        s_mt = sem("s_mt")
        s_mr = sem("s_mr")
        s_st = sem("s_st")
        s_ex = sem("s_ex")
        s_pv = sem("s_pv")
        s_or = sem("s_or")
        s_so = [sem(f"s_so{r}") for r in range(2)]
        s_rc = sem("s_rc")
        s_rb = sem("s_rb")
        s_sh = sem("s_sh")
        s_on = sem("s_on")
        s_oc = [sem(f"s_oc{r}") for r in range(2)]
        s_zero = sem("s_zero")
        s_zt = sem("s_zt")
        s_tail = sem("s_tail")
        s_zs = sem("s_zs")
        s_op, s_res, s_xn2, s_t2, s_t2e, s_lg = (sem(n) for n in ("s_op", "s_res", "s_xn2", "s_t2", "s_t2e", "s_lg"))
        s_lsh, s_lex, s_pick, s_rank, s_slot = (sem(n) for n in ("s_lsh", "s_lex", "s_pick", "s_rank", "s_slot"))
        s_scat = sem("s_scat")
        s_w13 = [sem(f"s_w13_{h}") for h in range(2)]
        s_w2 = sem("s_w2")
        s_hi13, s_lo13 = sem("s_hi13"), sem("s_lo13")
        s_hi2, s_lo2 = sem("s_hi2"), [sem(f"s_lo2_{h}") for h in range(2)]
        s_xg, s_xt, s_xh, s_xl = (sem(n) for n in ("s_xg", "s_xt", "s_xh", "s_xl"))
        s_up, s_silu, s_act = (sem(n) for n in ("s_up", "s_silu", "s_act"))
        s_at, s_ah, s_al = (sem(n) for n in ("s_at", "s_ah", "s_al"))
        s_down, s_ye, s_ys = (sem(n) for n in ("s_down", "s_ye", "s_ys"))
        s_g = [sem(f"s_g{t}") for t in range(NT)]
        s_half, s_fin, s_out = sem("s_half"), sem("s_fin"), sem("s_out")

        N_CONST = 7

        jobs = []
        for b in range(B):
            jobs += [("t", b, i) for i in range(TPB)]
            jobs += [(kind, b, i) for kind in "qk" for i in range(HC)]
            jobs += [("v", b, i) for i in range(TPB)]
        n_of = {j: n for n, j in enumerate(jobs)}
        a_count = [n + 1 for n in range(len(jobs))]
        d_count, c = [], 0
        for j in jobs:
            c += j[0] in "qk"
            d_count.append(c)

        def job_read(eng, n):
            if jobs[n][0] in "qk":
                eng.wait_ge(s_jd, d_count[n])
            eng.wait_ge(s_ja, a_count[n])

        def head_at(g, j):
            at = (g // 2) % RING
            return qs[at][:, j % 2, 2 * (g % 2) + j // 2, :], ks[at][:, 2 * (g % 2) + j // 2, :]

        def scores_at(u2):
            j, qt = divmod(u2, TPB)
            return j, qt, (j % 2) * 8 + (j // 2) * TPB + qt

        turns = []
        for s in range(-2, NG):
            turns += [(s + 2, u2) for u2 in range(2)]
            turns += [(s + 1, "maxima")] * (s + 1 >= 0)
            turns += [(s + 2, u2) for u2 in range(2, 4 * TPB)]
        turns = [t for t in turns if t[0] < NG]
        max_banks = [ps2[:, 0, :], ps2[:, 1, :], ps_m[:, :]]
        turn_of = {t: n for n, t in enumerate(turns)}

        def max_bank(g, what):
            return max_banks[turn_of[g, what] % 3]

        def max_bank_free(eng, g, what):
            n = turn_of[g, what] - 3
            if n >= 0:
                before, what = turns[n]
                if what == "maxima":
                    eng.wait_ge(s_mr, before + 1)
                else:
                    eng.wait_ge(s_mx, before * 16 + what + 1)

        block = ctx.enter_context(nc.Block())

        @block.sync
        def _(sp):
            x_t = x.rearrange("(n p) h -> p n h", p=P)
            sp.dma_start(x_sb[:, 0:TPB, :], x_t[:, 0:TPB, :]).then_inc(s_x[0], 16)
            sp.dma_start(wq_sb[:, :, :], wq.rearrange("p (c e) -> p c e", c=HC)).then_inc(s_wq, 16)
            sp.dma_start(wk_sb[:, :, :], wk.rearrange("p (c e) -> p c e", c=HC)).then_inc(s_wk, 16)
            sp.dma_start(x_sb[:, TPB:NT, :], x_t[:, TPB:NT, :]).then_inc(s_x[1], 16)
            sp.dma_start(wv_sb[:, :, :], wv.rearrange("p (c e) -> p c e", c=HC)).then_inc(s_wv, 16)
            sp.wait_ge(s_zero, 3)
            sp.dma_start(xs_dram.rearrange("(n p) h -> p n h", p=P),
                         rec_row[:, :].unsqueeze(1).broadcast_to([P, MT, HID])).then_inc(s_zs, 16)
            for s in range(-4, NG + 2):
                g = s + 1
                if 0 <= g < NG:
                    sp.wait_ge(s_mr, g + 1)
                    for par in range(2):
                        sp.dma_start(qs[(g // 2) % RING][MROW:MROW + 1, par, 2 * (g % 2):2 * (g % 2) + 2, :].bitcast(f32)
                                     .rearrange("a p (t c) -> a (p t) c", c=P),
                                     max_rows[8 * par:8 * par + 8, g % 2, :].bitcast(f32)).then_inc(s_row[g % 4], 16)
                g = s - 2
                if 0 <= g < NG:
                    sp.wait_ge(s_rc, g + 1)
                    if g >= 1:
                        sp.wait_ge(s_sh, g)
                    sp.dma_start(rec_row[1:P:2 * D, :], sum_rec[:, g % 2, :]).then_inc(s_rb, 16)
                g = s - 1
                if 0 <= g < NG:
                    sp.wait_ge(s_or, g + 1)
                    if g >= 2:
                        sp.wait_ge(s_rb, 16 * (g - 1))
                    sp.dma_start(sum_rec[:, g % 2, :], o_raw[1:P:2 * D, g % 2, :]).then_inc(s_so[g % 2], 16)
                pair = (s + 4) // 2
                if pair < NG // 2:
                    at = pair % RING
                    if s % 2 == 0:
                        sp.wait_ge(s_ones, 2 * min(pair + 1, RING))
                        if pair >= RING:
                            sp.wait_ge(s_st, UNITS * (2 * (pair - RING) + 2))
                        last = ("k", pair // HC, pair % HC)
                        sp.wait_ge(s_jd, d_count[n_of[last]])
                    par = s % 2
                    for part, (qsrc, ksrc) in enumerate(((q_hi, k_hi), (q_lo, k_hi), (q_hi, k_lo))):
                        dst = slice(64 * par + D * part, 64 * par + D * (part + 1))
                        for to, frm in ((qs[at][dst, par, :, :], qsrc), (ks[at][dst, :, :], ksrc)):
                            sp.dma_start(to.bitcast(f32),
                                         frm[64 * par:64 * par + 64, pair, :].bitcast(f32)).then_inc(s_stack[at], 16)
                g = s - 2
                if g >= 0:
                    sp.wait_ge(s_on, g + 1)
                    sp.dma_start(o_all[64 * (g % 2):64 * (g % 2) + 64, g // 2, :],
                                 o_norm[0:P:2, g % 2, :]).then_inc(s_oc[g % 2], 16)
                if g == 8:
                    sp.dma_start(wo_sb, wo.rearrange("p (c e) -> p c e", c=HC)).then_inc(s_wo, 16)
            sp.wait_ge(s_pv, TPB * NG)
            sp.wait_ge(s_on, NG)
            sp.dma_start(x1[:, :, :], x_t).then_inc(s_x[0], 16)
            sp.dma_start(gw_sb[:, :, :], gw.rearrange("p (c e) -> p c e", c=HC)).then_inc(s_gw, 16)

            def of_tile(i):
                return (sp.value_load(tile_i[0:1, bass.ds(i, 1)], min_val=0, max_val=E - 1),
                        sp.value_load(new_i[0:1, bass.ds(i, 1)], min_val=0, max_val=1))

            W13 = HC * F

            def load13(half, e, cond):
                sp.dma_start(w13_sb[:, 2 * half:2 * half + 2, :, :].rearrange("p q c f -> p (q c f)"),
                             w13[bass.ds(e, 1), :, half * W13:(half + 1) * W13].rearrange("a p n -> (a p) n"),
                             cond=cond).then_inc(s_w13[half], 16)

            def load2(e, cond):
                sp.dma_start(w2_sb[:, 0:FC - 1, :].rearrange("p c f -> p (c f)"),
                             w2[bass.ds(e, 1), :, :].rearrange("a p n -> (a p) n"), cond=cond).then_inc(s_w2, 16)
                sp.dma_start(w2_sb[0:FTAIL, FC - 1, :],
                             w2t[bass.ds(e, 1), :, :].rearrange("a p n -> (a p) n"), cond=cond).then_inc(s_w2, 16)

            def load_rows(i):
                sp.dma_start(xg[:, :], xs_dram[bass.ds(i * P, P), :]).then_inc(s_xg, 16)

            def store(i):
                sp.wait_ge(s_ye, i + 1)
                sp.dma_start(ys_dram[bass.ds(i * P, P), :], y_sb[:, :]).then_inc(s_ys, 16)

            def ahead13(i):
                e, new = of_tile(i)
                sp.wait_ge(s_lo13, 4 * i - 2)
                load13(0, e, new)
                sp.wait_ge(s_lo13, 4 * i)
                load13(1, e, new)
                sp.wait_ge(s_xt, i)
                load_rows(i)

            def ahead2(i):
                e, new = of_tile(i)
                for h in range(2):
                    sp.wait_ge(s_lo2[h], i)
                load2(e, new)

            for half in range(2):
                load13(half, 0, None)
            sp.wait_ge(s_tail, 1)
            load2(0, None)
            sp.wait_ge(s_slot, 1)
            e, new = of_tile(0)
            sp.wait_ge(s_w13[0], 16)
            sp.wait_ge(s_w13[1], 16)
            sp.wait_ge(s_w2, 32)
            for half in range(2):
                load13(half, e, new)
            load2(e, new)
            sp.wait_ge(s_scat, 16 * NT * TOPK)
            load_rows(0)
            ahead13(1)
            ahead13(2)
            ahead2(1)
            with sp.Fori(1, MT - 2) as i:
                ahead13(i + 2)
                ahead2(i + 1)
                store(i - 1)
            ahead2(MT - 1)
            for i in (MT - 3, MT - 2, MT - 1):
                store(i)
            for t in range(NT):
                sp.wait_ge(s_fin, t + 1)
                sp.dma_start(out[t * P:(t + 1) * P, :], x1[:, t, :]).then_inc(s_out, 16)
            sp.wait_ge(s_out, 16 * NT)

        @block.gpsimd
        def _(pool):
            pool.memset(ident[:, :], 0.0).then_inc(s_zero, 1)
            pool.memset(before_b[:, :], 1.0).then_inc(s_zero, 1)
            pool.memset(rec_row[:, :], 0.0).then_inc(s_zero, 1)
            pool.wait_ge(s_zero, 3)
            pool.affine_select(out=ident[:, :], in_=ident[:, :], compare_op=ALU.not_equal, fill=1.0,
                               base=0, pattern=[[-1, P]], channel_multiplier=1).then_inc(s_const, 1)
            pool.affine_select(out=before_b[:, :], in_=before_b[:, :], compare_op=ALU.is_gt, fill=0.0,
                               base=0, pattern=[[1, P]], channel_multiplier=-1).then_inc(s_const, 1)
            pool.memset(ones_b[:, :], 1.0).then_inc(s_const, 1)
            pool.memset(v_ones[:, :, :, :, 1], 1.0).then_inc(s_const, 1)

            def prepare(r):
                pool.memset(qs[r][:, :, :, :].bitcast(f32), 0.0).then_inc(s_ones, 1)
                pool.memset(ks[r][:, :, :].bitcast(f32), 1.0).then_inc(s_ones, 1)

            prepare(0)
            pool.iota(e_of[:, :, :], pattern=[[0, NT], [1, E]], base=0, channel_multiplier=0,
                      allow_small_or_imprecise_dtypes=True).then_inc(s_const, 1)
            pool.iota(tile_of[:, :, :], pattern=[[1, MT], [0, E]], base=0, channel_multiplier=0,
                      allow_small_or_imprecise_dtypes=True).then_inc(s_const, 1)
            pool.memset(e_before[:, :, :], 1.0).then_inc(s_zt, 1)
            pool.wait_ge(s_zt, 1)
            pool.affine_select(out=e_before[:, :, :], in_=e_before[:, :, :], compare_op=ALU.is_gt, fill=0.0,
                               base=0, pattern=[[1, E], [-1, E]], channel_multiplier=0).then_inc(s_const, 1)
            pool.wait_ge(s_job, n_of[("t", 1, TPB - 1)] + 1)
            prepare(1)
            pool.wait_ge(s_job, len(jobs))
            prepare(2)
            for g in range(NG):
                pool.wait_ge(s_sh, g + 1)
                if g >= 2:
                    pool.wait_ge(s_oc[g % 2], 16 * (g // 2))
                pool.tensor_tensor(o_norm[:, g % 2, :], o_raw[:, g % 2, :], rec_all[:, :],
                                   ALU.mult).then_inc(s_on, 1)
            pool.wait_ge(s_pv, TPB * NG)
            pool.memset(w2_sb[:, FC - 1, :], 0.0).then_inc(s_tail, 1)
            pool.wait_ge(s_zs, 16)
            pool.wait_ge(s_slot, 1)
            for t in range(NT):
                for k in range(TOPK):
                    pool.indirect_dma_start(
                        out=xs_dram[:, :], out_offset=bass.IndirectOffsetOnAxis(ap=slot_i[:, k, t:t + 1], axis=0),
                        in_=xn2[:, t, :], in_offset=None).then_inc(s_scat, 16)

            def w2_split(i):
                pool.wait_ge(s_hi2, 2 * i + 2)
                pool.tensor_tensor(w2_lo[:, FC // 2:FC, :], w2_sb[:, FC // 2:FC, :],
                                   w2_hi[:, FC // 2:FC, :].bitcast(f32), ALU.subtract).then_inc(s_lo2[1], 1)

            w2_split(0)
            with pool.Fori(1, MT) as i:
                pool.wait_ge(s_down, 2 * i)
                w2_split(i)
            pool.wait_ge(s_ys, 16 * MT)
            for t in range(NT):
                for k in range(TOPK):
                    pool.indirect_dma_start(
                        out=gathered[k][:, t, :], out_offset=None, in_=ys_dram[:, :],
                        in_offset=bass.IndirectOffsetOnAxis(ap=slot_i[:, k, t:t + 1], axis=0)).then_inc(s_g[t], 16)

        @block.tensor
        def _(pe):
            pe.wait_ge(s_const, N_CONST)
            for n, (kind, b, i) in enumerate(jobs):
                if n >= NB:
                    job_read(pe, n - NB)
                o = banks[n % NB]
                if kind == "t":
                    pe.wait_ge(s_xn, b * TPB + i + 1)
                    for c in range(HC):
                        last = pe.transpose(o[:, c * P:(c + 1) * P], xn_sb[:, i, c * P:(c + 1) * P], ident[:, :])
                elif kind in "qk":
                    w = wq_sb if kind == "q" else wk_sb
                    pe.wait_ge(s_wq if kind == "q" else s_wk, 16)
                    pe.wait_ge(s_ja, a_count[n_of[("t", b, TPB - 1)]])
                    for c in range(HC):
                        last = pe.matmul(o, w[:, c, i * P:(i + 1) * P], xnT[:, c, b * S:(b + 1) * S],
                                         start=(c == 0), stop=(c == HC - 1))
                else:
                    pe.wait_ge(s_wv, 16)
                    t0 = b * S + i * P
                    for c in range(HC):
                        last = pe.matmul(o, xnT[:, c, t0:t0 + P], wv_sb[:, c, :],
                                         start=(c == 0), stop=(c == HC - 1))
                last.then_inc(s_job, 1)
            for n in range(len(jobs) - NB, len(jobs)):
                job_read(pe, n)

            def pv(g, kc):
                if not 0 <= g < NG:
                    return
                pe.wait_ge(s_ex, UNITS * g + 2 * (kc + 1))
                if kc == 0 and g >= 1:
                    pe.wait_ge(s_or, g)
                for j in range(GH):
                    last = pe.matmul(ps_o[32 * j:32 * j + 32, :],
                                     v_ones[:, (g // 8) * TPB + kc, (g % 8) * GH + j, :, :].rearrange("p d o -> p (d o)"),
                                     probs_t[:, kc % 2, j, :], start=(kc == 0), stop=(kc == TPB - 1),
                                     tile_position=(0, 32 * j))
                last.then_inc(s_pv, 1)

            def max_t(g):
                pe.wait_ge(s_mx, 16 * (g + 1))
                max_bank_free(pe, g, "maxima")
                pe.transpose(max_bank(g, "maxima")[0:4 * GH, 0:P], neg_max[:, g % 2, :], ident[:, :]).then_inc(s_mt, 1)

            def key_max(g, u2):
                if g >= NG:
                    return
                j, qt, _ = scores_at(u2)
                q, k = head_at(g, j)
                max_bank_free(pe, g, u2)
                pe.matmul(max_bank(g, u2), q[0:MROW, qt * P:(qt + 1) * P],
                          k[0:MROW, :], start=True, stop=True).then_inc(s_sn, 1)

            def scores(g, u):
                if not 0 <= g < NG:
                    return
                n = g * UNITS + u
                if n >= 2:
                    pe.wait_ge(s_ex, n - 1)
                kc, half = divmod(u, 2)
                for c in range(2):
                    q, k = head_at(g, 2 * half + c)
                    last = pe.matmul(ps4[:, 2 * (n % 2) + c, :], k[0:MROW + 1, kc * P:(kc + 1) * P],
                                     q[0:MROW + 1, :], start=True, stop=True)
                last.then_inc(s_st, 1)

            for s in range(-2, NG + 1):
                ga = s + 2
                if ga < NG and ga % 2 == 0:
                    pe.wait_ge(s_stack[(ga // 2) % RING], 16 * 12 * (ga // 2 // RING + 1))
                if 0 <= s < NG:
                    pe.wait_ge(s_row[s % 4], 32 * (s // 4 + 1))
                for p in range(TPB):
                    key_max(ga, 4 * p)
                    key_max(ga, 4 * p + 1)
                    if p < 2:
                        pv(s - 1, p + 2)
                    else:
                        pv(s, p - 2)
                    if p == 0 and 0 <= s + 1 < NG:
                        max_t(s + 1)
                    key_max(ga, 4 * p + 2)
                    scores(s, 2 * p)
                    key_max(ga, 4 * p + 3)
                    scores(s, 2 * p + 1)

            pe.wait_ge(s_wo, 16)
            for r in range(2):
                pe.wait_ge(s_oc[r], 16 * NG // 2)
            for t in range(NT):
                if t >= 4:
                    pe.wait_ge(s_res, t - 3)
                b, qt = divmod(t, TPB)
                for c in range(HC):
                    last = pe.matmul(ps4[:, t % 4, :], o_all[:, b * HC + c, qt * P:(qt + 1) * P], wo_sb[:, c, :],
                                     start=(c == 0), stop=(c == HC - 1))
                last.then_inc(s_op, 1)
            pe.wait_ge(s_gw, 16)
            for t in range(NT):
                pe.wait_ge(s_xn2, t + 1)
                if t >= 2:
                    pe.wait_ge(s_t2e, t - 1)
                for c in range(HC):
                    last = pe.transpose(ps2[:, t % 2, c * P:(c + 1) * P], xn2[:, t, c * P:(c + 1) * P], ident[:, :])
                last.then_inc(s_t2, 1)
                pe.wait_ge(s_t2e, t + 1)
                for c in range(HC):
                    last = pe.matmul(ps_o[:, t * E:(t + 1) * E], xn2T[:, t % 2, c, :], gw_sb[:, c, :],
                                     start=(c == 0), stop=(c == HC - 1))
                last.then_inc(s_lg, 1)
            pe.wait_ge(s_pick, 1)
            pk = picks[:, :, :].rearrange("p t e -> p (t e)")
            for d in range(1, NT):
                pe.matmul(ps_m[:, d * E:NT * E], ones_b[:, :], pk[:, 0:(NT - d) * E],
                          start=(d == 1), stop=False, skip_group_check=True)
            pe.matmul(ps_m[:, 0:NT * E], before_b[:, :], pk, start=False, stop=True, skip_group_check=True)
            for t in range(NT):
                last = pe.matmul(ps2[:, 0, 0:E], ones_b[:, :], pk[:, t * E:(t + 1) * E],
                                 start=(t == 0), stop=(t == NT - 1))
            last.then_inc(s_rank, 1)

            def rows_in(i):
                pe.wait_ge(s_xg, 16 * (i + 1))
                for c in range(HC):
                    last = pe.transpose(ps_m[:, c * P:(c + 1) * P], xg[:, c * P:(c + 1) * P], ident[:, :])
                last.then_inc(s_xt, 1)

            def three(o, x_hi, x_lo, w_hi, w_lo, start, stop):
                pe.matmul(o, x_hi, w_hi, start=start, stop=False)
                pe.matmul(o, x_hi, w_lo, start=False, stop=False)
                return pe.matmul(o, x_lo, w_hi, start=False, stop=stop)

            def up(i):
                pe.wait_ge(s_xl, i + 1)
                for q in range(4):
                    pe.wait_ge(s_lo13, 4 * i + q + 1)
                    if not (isinstance(i, int) and i == 0) and q in (0, 2):
                        pe.wait_ge((s_silu, s_act)[q // 2], i)
                    for c in range(HC):
                        last = three(ps4[:, q, 0:FH], xgT_hi[:, c, :], xgT_lo[:, c, :], w13_hi[:, q, c, :],
                                     w13_lo[:, q, c, :], c == 0, c == HC - 1)
                    last.then_inc(s_up, 1)

            def down(i):
                pe.wait_ge(s_al, i + 1)
                if not (isinstance(i, int) and i == 0):
                    pe.wait_ge(s_ye, i)
                for c in range(FC):
                    if c in (0, FC // 2):
                        pe.wait_ge(s_lo2[c // (FC // 2)], i + 1)
                    k = P if c < FC - 1 else FTAIL
                    last = three(ps_o[:, :], actT_hi[0:k, c, :], actT_lo[0:k, c, :], w2_hi[0:k, c, :],
                                 w2_lo[0:k, c, :], c == 0, c == FC - 1)
                    if c in (FC // 2 - 1, FC - 1):
                        last.then_inc(s_down, 1)

            def inner_t(i):
                pe.wait_ge(s_act, i + 1)
                for c in range(FC):
                    k = P if c < FC - 1 else FTAIL
                    last = pe.transpose(ps2[0:k, c // 4, (c % 4) * P:(c % 4 + 1) * P],
                                        act[:, c * P:c * P + k], ident[:, :])
                last.then_inc(s_at, 1)

            rows_in(0)
            up(0)
            rows_in(1)
            inner_t(0)
            with pe.Fori(1, MT - 1) as i:
                up(i)
                rows_in(i + 1)
                down(i - 1)
                inner_t(i)
            up(MT - 1)
            down(MT - 2)
            inner_t(MT - 1)
            down(MT - 1)

        @block.scalar
        def _(a):
            def root(n, t0):
                a.wait_ge(s_var, n)
                a.activation(rstd[:, t0:t0 + TPB], rstd[:, t0:t0 + TPB], ACT.Sqrt).then_inc(s_std, 1)

            for b in range(B):
                root(b + 1, b * TPB)
            for n, (kind, b, i) in enumerate(jobs):
                o = banks[n % NB]
                a.wait_ge(s_job, n + 1)
                if kind == "t":
                    t0 = b * S + i * P
                    a.activation(xnT[:, :, t0:t0 + P], o.rearrange("p (c t) -> p c t", c=HC), ACT.Copy).then_inc(s_ja, 1)
                elif kind == "v":
                    a.activation(v_ones[:, b * TPB + i, :, :, 0], o.rearrange("p (h d) -> p h d", d=D),
                                 ACT.Copy).then_inc(s_ja, 1)
                else:
                    hi = q_hi if kind == "q" else k_hi
                    a.activation(hi[:, b * HC + i, :], o, ACT.Copy).then_inc(s_ja, 1)
            for s in range(-2, NG + 1):
                for u in range(UNITS):
                    g = s + 1
                    if u == 0 and 0 <= g < NG:
                        a.wait_ge(s_mt, g + 1)
                        if g >= 2:
                            a.wait_ge(s_row[(g - 2) % 4], 32 * ((g - 2) // 4 + 1))
                        a.activation(max_rows[:, g % 2, :], max_bank(g, "maxima")[0:4 * GH, 0:P],
                                     ACT.Copy).then_inc(s_mr, 1)
                    g = s - 1
                    if u == 2 and g >= 0:
                        a.wait_ge(s_pv, TPB * (g + 1))
                        if g >= 2:
                            a.wait_ge(s_so[g % 2], 16 * (g // 2))
                            a.wait_ge(s_on, g - 1)
                        a.activation(o_raw[:, g % 2, :], ps_o[:, :], ACT.Copy).then_inc(s_or, 1)
                    if 0 <= s < NG:
                        n = s * UNITS + u
                        kc, half = divmod(u, 2)
                        m = s * TPB + kc
                        if m >= 2 and half == 0:
                            a.wait_ge(s_pv, m - 1)
                        a.wait_ge(s_st, n + 1)
                        a.activation(probs_t[:, kc % 2, 2 * half:2 * half + 2, :], ps4[:, 2 * (n % 2):2 * (n % 2) + 2, :],
                                     ACT.Exp, scale=D ** -0.5).then_inc(s_ex, 1)
            for t in range(NT):
                if t % TPB == 0:
                    root(B + t // TPB + 1, t)
                a.wait_ge(s_t2, t + 1)
                if t >= 2:
                    a.wait_ge(s_lg, t - 1)
                a.activation(xn2T[:, t % 2, :, :], ps2[:, t % 2, :].rearrange("p (c t) -> p c t", c=HC),
                             ACT.Copy).then_inc(s_t2e, 1)
            a.wait_ge(s_lsh, 1)
            a.activation(pe_[:, :, :], lsh[:, :, :], ACT.Exp).then_inc(s_lex, 1)

            def split13(i, q):
                a.wait_ge(s_w13[q // 2], 16 * (i + 2))
                if not (isinstance(i, int) and i == 0):
                    a.wait_ge(s_up, 4 * i + q - 3)
                a.activation(w13_hi[:, q, :, :], w13_sb[:, q, :, :], ACT.Copy).then_inc(s_hi13, 1)

            def split2(i, h):
                a.wait_ge(s_w2, 32 * (i + 2))
                if not (isinstance(i, int) and i == 0):
                    a.wait_ge(s_down, 2 * i + h - 1)
                c = slice(FC // 2, FC) if h else slice(0, FC // 2)
                a.activation(w2_hi[:, c, :], w2_sb[:, c, :], ACT.Copy).then_inc(s_hi2, 1)

            def silu(i):
                a.wait_ge(s_up, 4 * i + 2)
                if not (isinstance(i, int) and i == 0):
                    a.wait_ge(s_act, i)
                a.activation(gate[:, :].rearrange("p (h f) -> p h f", h=2), ps4[:, 0:2, 0:FH],
                             ACT.Silu).then_inc(s_silu, 1)

            def rows_hi(i):
                a.wait_ge(s_xt, i + 1)
                if not (isinstance(i, int) and i == 0):
                    a.wait_ge(s_up, 4 * i)
                a.activation(xgT_hi[:, :, :].rearrange("p c t -> p (c t)"), ps_m[:, :], ACT.Copy).then_inc(s_xh, 1)

            def inner_hi(i):
                a.wait_ge(s_at, i + 1)
                if not (isinstance(i, int) and i == 0):
                    a.wait_ge(s_down, 2 * i)
                a.activation(actT_hi[:, 0:4, :].rearrange("p c t -> p (c t)"), ps2[:, 0, :], ACT.Copy)
                a.activation(actT_hi[:, 4:6, :].rearrange("p c t -> p (c t)"), ps2[:, 1, 0:2 * P], ACT.Copy)
                a.activation(actT_hi[0:FTAIL, FC - 1, :], ps2[0:FTAIL, 1, 2 * P:3 * P], ACT.Copy).then_inc(s_ah, 1)

            def y_out(i):
                a.wait_ge(s_down, 2 * i + 2)
                if not (isinstance(i, int) and i == 0):
                    a.wait_ge(s_ys, 16 * i)
                a.activation(y_sb[:, :], ps_o[:, :], ACT.Copy).then_inc(s_ye, 1)

            for q in range(4):
                split13(0, q)
            rows_hi(0)
            split13(1, 0)
            split13(1, 1)
            silu(0)
            split13(1, 2)
            split13(1, 3)
            rows_hi(1)
            split2(0, 0)
            split2(0, 1)
            inner_hi(0)
            with a.Fori(1, MT - 1) as i:
                split13(i + 1, 0)
                split13(i + 1, 1)
                silu(i)
                split13(i + 1, 2)
                split13(i + 1, 3)
                rows_hi(i + 1)
                split2(i, 0)
                y_out(i - 1)
                split2(i, 1)
                inner_hi(i)
            silu(MT - 1)
            split2(MT - 1, 0)
            y_out(MT - 2)
            split2(MT - 1, 1)
            inner_hi(MT - 1)
            y_out(MT - 1)

        @block.vector
        def _(v):
            chain, norms = [0], [0]

            def link(ins):
                chain[0] += 1
                ins.then_inc(s_dve, 1)
                v.wait_ge(s_dve, chain[0])

            def norm(src, dst, t0, n, done, free):
                for t in range(t0, t0 + n):
                    ins = v.bn_stats(stats[:, t, :], src[:, t, :])
                link(ins)
                for t in range(t0, t0 + n):
                    ins = v.bn_aggr(aggr[:, t, :], stats[:, t, :])
                link(ins)
                v.tensor_scalar(rstd[:, t0:t0 + n], aggr[:, t0:t0 + n, 1], EPS, None, ALU.add).then_inc(s_var, 1)
                norms[0] += 1
                v.wait_ge(s_std, norms[0])
                link(v.reciprocal(rstd[:, t0:t0 + n], rstd[:, t0:t0 + n]))
                if free is not None:
                    v.wait_ge(s_job, free)
                for k in range(n):
                    t = t0 + k
                    v.tensor_scalar(dst(t), src[:, t, :], aggr[:, t, 0:1], rstd[:, t:t + 1],
                                    ALU.subtract, ALU.mult).then_inc(done, 1)

            for b in range(B):
                v.wait_ge(s_x[b], 16)
                norm(x_sb, lambda t: xn_sb[:, t % TPB, :], b * TPB, TPB, s_xn, n_of[("t", 0, TPB - 1)] + 1 if b else None)
            for n, (kind, b, i) in enumerate(jobs):
                if kind in "qk":
                    hi, lo = (q_hi, q_lo) if kind == "q" else (k_hi, k_lo)
                    v.wait_ge(s_ja, a_count[n])
                    v.tensor_tensor(lo[:, b * HC + i, :], banks[n % NB], hi[:, b * HC + i, :].bitcast(f32),
                                    ALU.subtract).then_inc(s_jd, 1)
            for s in range(-2, NG + 2):
                ga = s + 2
                if 2 <= ga < NG:
                    v.wait_ge(s_mt, ga - 1)
                for u2 in range(16):
                    if ga < NG:
                        _, _, col = scores_at(u2)
                        n = ga * 16 + u2
                        v.wait_ge(s_sn, n + 1)
                        v.tensor_reduce(neg_max[:, ga % 2, col:col + 1], max_bank(ga, u2), AX.X, ALU.max,
                                        negate=True).then_inc(s_mx, 1)
                    g = s - 2
                    if u2 == 1 and g >= 0:
                        v.wait_ge(s_so[g % 2], 16 * (g // 2 + 1))
                        v.reciprocal(sum_rec[:, g % 2, :], sum_rec[:, g % 2, :]).then_inc(s_rc, 1)
                    if u2 == 11 and g >= 0:
                        v.wait_ge(s_rb, 16 * (g + 1))
                        if g >= 1:
                            v.wait_ge(s_on, g)
                        v.stream_shuffle(rec_all[:, :], rec_row[:, :], [1] * 32).then_inc(s_sh, 1)
            v.wait_ge(s_x[0], 32)
            for t in range(NT):
                v.wait_ge(s_op, t + 1)
                ins = v.tensor_tensor(x1[:, t, :], ps4[:, t % 4, :], x1[:, t, :], ALU.add).then_inc(s_res, 1)
                if t % TPB == TPB - 1:
                    v.wait_ge(s_res, t + 1)
                    norm(x1, lambda t: xn2[:, t, :], t + 1 - TPB, TPB, s_xn2, None)
            v.wait_ge(s_lg, NT)
            v.wait_ge(s_const, N_CONST)
            lg = ps_o[:, 0:NT * E].rearrange("p (t e) -> p t e", e=E)
            wide = lambda a: a.unsqueeze(2).broadcast_to([P, NT, E])
            link(v.tensor_reduce(lmax[:, :], lg, AX.X, ALU.max))
            v.tensor_tensor(lsh[:, :, :], lg, wide(lmax[:, :]), ALU.subtract).then_inc(s_lsh, 1)
            v.wait_ge(s_lex, 1)
            link(v.tensor_reduce(psums[:, :], pe_[:, :, :], AX.X, ALU.add))
            link(v.reciprocal(prec[:, :], psums[:, :]))
            link(v.tensor_tensor(pr[:, :, :], pe_[:, :, :], wide(prec[:, :]), ALU.mult))
            for t in range(NT):
                ins = v.max(top[:, t, :], pr[:, t, :])
            link(ins)
            for t in range(NT):
                ins = v.max_index(top_i[:, t, :], top[:, t, :], pr[:, t, :])
            link(ins)
            v.tensor_reduce(wsum[:, :], top[:, :, 0:TOPK], AX.X, ALU.add)
            link(v.tensor_copy(top_f[:, :, :], top_i[:, :, :]))
            v.reciprocal(wrec[:, :], wsum[:, :])
            for k in range(TOPK):
                ins = v.tensor_tensor(pick[:, k, :, :], e_of[:, :, :], wide(top_f[:, :, k]), ALU.is_equal)
            link(ins)
            v.tensor_tensor(picks[:, :, :], pick[:, 0, :, :], pick[:, 1, :, :], ALU.add).then_inc(s_pick, 1)
            for k in range(TOPK):
                v.tensor_tensor(wtok[:, k, :], top[:, :, k], wrec[:, :], ALU.mult)
            v.wait_ge(s_rank, 1)
            link(v.tensor_scalar(n_i[:, :], ps2[:, 0, 0:E], float(P - 1), None, ALU.add))
            link(v.tensor_scalar(c_i[:, :], n_i[:, :], 7, None, ALU.arith_shift_right))
            link(v.tensor_copy(c_f[:, :], c_i[:, :]))
            link(v.tensor_tensor(c_bef[:, :, :], e_before[:, :, :],
                                 c_f[:, :].unsqueeze(1).broadcast_to([P, E, E]), ALU.mult))
            link(v.tensor_reduce(first[:, :], c_bef[:, :, :], AX.X, ALU.add))
            v.scalar_tensor_tensor(slot_e[:, :, :], first[:, :].unsqueeze(1).broadcast_to([P, NT, E]), float(P),
                                   ps_m[:, 0:NT * E].rearrange("p (t e) -> p t e", e=E), ALU.mult, ALU.add)
            link(v.tensor_tensor(ends[:, :], first[:, :], c_f[:, :], ALU.add))
            for k in range(TOPK):
                v.tensor_tensor(slot_p[:, k, :, :], pick[:, k, :, :], slot_e[:, :, :], ALU.mult)
            link(v.tensor_tensor(passed[:, :, :], ends[:, :].unsqueeze(1).broadcast_to([P, MT, E]),
                                 tile_of[:, :, :], ALU.is_le))
            v.tensor_reduce(slot_f[:, :, :], slot_p[:, :, :, :], AX.X, ALU.add)
            link(v.tensor_reduce(tile_f[:, :], passed[:, :, :], AX.X, ALU.add))
            v.tensor_copy(slot_i[:, :, :], slot_f[:, :, :])
            link(v.tensor_scalar(tile_f[:, :], tile_f[:, :], float(E - 1), None, ALU.min))
            v.tensor_copy(tile_i[:, :], tile_f[:, :])
            v.tensor_copy(new_f[:, 0:1], tile_f[:, 0:1])
            link(v.tensor_tensor(new_f[:, 1:MT], tile_f[:, 1:MT], tile_f[:, 0:MT - 1], ALU.subtract))
            v.tensor_scalar(new_i[:, :], new_f[:, :], 0.0, None, ALU.is_gt).then_inc(s_slot, 1)

            def split13(i, q):
                v.wait_ge(s_hi13, 4 * i + q + 1)
                if not (isinstance(i, int) and i == 0):
                    v.wait_ge(s_up, 4 * i + q - 3)
                v.tensor_tensor(w13_lo[:, q, :, :], w13_sb[:, q, :, :], w13_hi[:, q, :, :].bitcast(f32),
                                ALU.subtract).then_inc(s_lo13, 1)

            def split2(i):
                v.wait_ge(s_hi2, 2 * i + 1)
                if not (isinstance(i, int) and i == 0):
                    v.wait_ge(s_down, 2 * i - 1)
                v.tensor_tensor(w2_lo[:, 0:FC // 2, :], w2_sb[:, 0:FC // 2, :], w2_hi[:, 0:FC // 2, :].bitcast(f32),
                                ALU.subtract).then_inc(s_lo2[0], 1)

            def rows_lo(i):
                v.wait_ge(s_xh, i + 1)
                if not (isinstance(i, int) and i == 0):
                    v.wait_ge(s_up, 4 * i)
                v.tensor_tensor(xgT_lo[:, :, :].rearrange("p c t -> p (c t)"), ps_m[:, :],
                                xgT_hi[:, :, :].rearrange("p c t -> p (c t)").bitcast(f32), ALU.subtract).then_inc(s_xl, 1)

            def gated(i):
                v.wait_ge(s_silu, i + 1)
                v.wait_ge(s_up, 4 * i + 4)
                if not (isinstance(i, int) and i == 0):
                    v.wait_ge(s_at, i)
                v.tensor_tensor(act[:, :].rearrange("p (h f) -> p h f", h=2), gate[:, :].rearrange("p (h f) -> p h f", h=2),
                                ps4[:, 2:4, 0:FH], ALU.mult).then_inc(s_act, 1)

            def inner_lo(i):
                v.wait_ge(s_ah, i + 1)
                if not (isinstance(i, int) and i == 0):
                    v.wait_ge(s_down, 2 * i)
                for k, c0, c1, bank in ((P, 0, 4, 0), (P, 4, 6, 1), (FTAIL, 6, 7, 1)):
                    at = (c0 % 4) * P
                    last = v.tensor_tensor(actT_lo[0:k, c0:c1, :].rearrange("p c t -> p (c t)"),
                                           ps2[0:k, bank, at:at + (c1 - c0) * P],
                                           actT_hi[0:k, c0:c1, :].rearrange("p c t -> p (c t)").bitcast(f32), ALU.subtract)
                last.then_inc(s_al, 1)

            for q in range(4):
                split13(0, q)
            rows_lo(0)

            def step(i, more=True):
                if more:
                    for q in range(3):
                        split13(i + 1, q)
                gated(i)
                if more:
                    split13(i + 1, 3)
                    rows_lo(i + 1)
                split2(i)
                inner_lo(i)

            step(0)
            with v.Fori(1, MT - 1) as i:
                step(i)
            step(MT - 1, more=False)
            for t in range(NT):
                v.wait_ge(s_g[t], 16 * TOPK)
                v.scalar_tensor_tensor(x1[:, t, :], gathered[0][:, t, :], wtok[:, 0, t:t + 1], x1[:, t, :],
                                       ALU.mult, ALU.add).then_inc(s_half, 1)
                v.wait_ge(s_half, t + 1)
                v.scalar_tensor_tensor(x1[:, t, :], gathered[1][:, t, :], wtok[:, 1, t:t + 1], x1[:, t, :],
                                       ALU.mult, ALU.add).then_inc(s_fin, 1)


def kernel(L0_attn_x, L0_attn_w_q, L0_attn_w_k, L0_attn_w_v, L0_attn_w_o,
           L0_ffn_gate_w, L0_ffn_w1, L0_ffn_w2, L0_ffn_w3):
    import numpy as np
    import concourse.bacc as bacc
    from concourse.bass_utils import run_bass_kernel_spmd

    def rows_first(w_t):
        r, n = w_t.shape
        return np.ascontiguousarray(w_t.reshape(r // P, P, n).transpose(1, 0, 2).reshape(P, -1))

    order = np.array([(8 * c + 4 * half + 2 * p + par) * D + d for c in range(HC)
                      for par in range(2) for d in range(D) for half in range(2) for p in range(2)])
    w1, w2, w3 = (np.asarray(w) for w in (L0_ffn_w1, L0_ffn_w2, L0_ffn_w3))
    w13 = np.concatenate([w1, w3], axis=1).transpose(0, 2, 1)
    w13 = np.ascontiguousarray(w13.reshape(E, HC, P, 4, FH).transpose(0, 2, 3, 1, 4).reshape(E, P, -1))
    w2_t = w2.transpose(0, 2, 1)
    main = (FC - 1) * P
    w2_main = np.ascontiguousarray(
        w2_t[:, :main, :].reshape(E, FC - 1, P, HID).transpose(0, 2, 1, 3).reshape(E, P, -1))
    arrays = {
        "x": np.asarray(L0_attn_x).reshape(T, HID),
        "wq": rows_first(np.asarray(L0_attn_w_q).T[:, order]),
        "wk": rows_first(np.asarray(L0_attn_w_k).T[:, order]),
        "wv": rows_first(np.asarray(L0_attn_w_v).T),
        "wo": rows_first(np.asarray(L0_attn_w_o).T),
        "gw": rows_first(np.asarray(L0_ffn_gate_w).T),
        "w13": w13,
        "w2": w2_main,
        "w2t": np.ascontiguousarray(w2_t[:, main:, :]),
    }
    nc = bacc.Bacc("TRN2", target_bir_lowering=False, num_devices=1)
    args = [nc.dram_tensor(k, a.shape, mybir.dt.from_np(a.dtype), kind="ExternalInput").ap() for k, a in arrays.items()]
    args.append(nc.dram_tensor("out", (T, HID), mybir.dt.float32, kind="ExternalOutput").ap())
    moe_layer(nc, *args)
    r = run_bass_kernel_spmd(nc, [arrays], core_ids=[0])
    return r.results[0]["out"].reshape(B, S, HID)
```

```python
import concourse.bass as bass
from concourse import mybir
from contextlib import ExitStack

P = 128
B, S, HID = 2, 512, 512
NH, D = 32, 16
T = B * S
NT = T // P
TPB = S // P
HC = HID // P
E, F, TOPK = 8, 800, 2
FH = F // 2
FC = -(-F // P)
FTAIL = F - (FC - 1) * P
STACK = 3 * FTAIL
GH = 4
NG = B * NH // GH
UNITS = 8
PROD = 3
ROWS = PROD * D
MROW = 64 + ROWS
RING = 3
MT = (T * TOPK - E) // P + E
LT = T * TOPK // P
PARTS = 5
EPS = 1e-5


def moe_layer(nc: bass.Bass, x, wq, wk, wv, wo, gw, w13, w2, w2t, out):
    f32, f32r, bf16 = mybir.dt.float32, mybir.dt.float32r, mybir.dt.bfloat16
    i32, u32 = mybir.dt.int32, mybir.dt.uint32
    ALU, ACT, AX = mybir.AluOpType, mybir.ActivationFunctionType, mybir.AxisListType

    xn2_dram = nc.dram_tensor("xn2_rows", [T, HID], f32, kind="Internal").ap()

    ctx = ExitStack()
    with ctx:
        def sem(name):
            return ctx.enter_context(nc.semaphore(name))

        def sb(c, name, shape, dt=f32):
            return c.enter_context(nc.sbuf_tensor(name, shape, dt))

        ident = sb(ctx, "ident", [P, P])
        ones_b = sb(ctx, "ones_b", [P, P], bf16)
        before_b = sb(ctx, "before_b", [P, P], bf16)
        stats = sb(ctx, "stats", [P, NT, 6])
        aggr = sb(ctx, "aggr", [P, NT, 2])
        rstd = sb(ctx, "rstd", [P, NT])
        neg_max = sb(ctx, "neg_max", [P, 2, 4 * GH])
        max_rows = sb(ctx, "max_rows", [4 * GH, 2, P], f32r)
        e_of = sb(ctx, "e_of", [P, NT, E])
        e_before = sb(ctx, "e_before", [P, E, E])
        tile_of = sb(ctx, "tile_of", [P, MT, E])
        row_i = sb(ctx, "row_i", [P, P], i32)
        token_parts = sb(ctx, "token_parts", [P, 2, TOPK, NT])
        dump_1 = sb(ctx, "dump_1", [P, 1])
        gw_sb = sb(ctx, "gw_sb", [P, HC, E])

        proj = ExitStack()
        q_hi = sb(proj, "q_hi", [P, NT, S], f32r)
        q_lo = sb(proj, "q_lo", [P, NT, S], f32r)
        k_hi = sb(proj, "k_hi", [P, NT, S], f32r)
        k_lo = sb(proj, "k_lo", [P, NT, S], f32r)
        o_all = q_hi[:, :, :].bitcast(f32)
        wo_sb = q_lo[:, 0:HC, :].bitcast(f32)
        w_raw = [t[:, HC:2 * HC, :].bitcast(f32) for t in (q_lo, k_lo, k_hi)]

        att = ExitStack()
        q_shape, k_shape = [P, 2, 4, S], [P, 4, S]
        q0 = sb(att, "q_stack0", q_shape, f32r)
        k0 = sb(att, "k_stack0", k_shape, f32r)
        v_ones = sb(att, "v_ones", [P, NT, NH, D, 2])
        sum_rec = sb(att, "sum_rec", [P, 2, GH * S // P])
        rec_row = sb(att, "rec_row", [P, S])
        pro = ExitStack()
        w_hi, w_lo = zip(*((sb(pro, f"w{n}_hi", [P, HC, HID], f32r), sb(pro, f"w{n}_lo", [P, HC, HID], f32r))
                           for n in "qkv"))
        pro.close()
        q1 = sb(att, "q_stack1", q_shape, f32r)
        k1 = sb(att, "k_stack1", k_shape, f32r)
        q2 = sb(att, "q_stack2", q_shape, f32r)
        k2 = sb(att, "k_stack2", k_shape, f32r)
        qs, ks = (q0, q1, q2), (k0, k1, k2)
        pro = ExitStack()
        x_sb = sb(pro, "x_sb", [P, NT, HID])
        xnT_hi = sb(pro, "xnT_hi", [P, HC, S], f32r)
        xnT_lo = sb(pro, "xnT_lo", [P, HC, S], f32r)
        pro.close()
        probs_t = sb(att, "probs_t", [P, 2, GH, S])
        o_raw = sb(att, "o_raw", [P, 2, S])
        rec_all = sb(att, "rec_all", [P, S])
        o_norm = sb(att, "o_norm", [P, 2, S])
        att.close()
        proj.close()

        w13_hi = sb(ctx, "w13_hi", [P, 4, HC, FH], f32r)
        w13_lo = sb(ctx, "w13_lo", [P, 4, HC, FH], f32r)
        w2_hi = sb(ctx, "w2_hi", [P, FC, HID], f32r)
        x1 = sb(ctx, "x1", [P, NT, HID])
        xn2 = sb(ctx, "xn2", [P, NT, HID])
        xn2T = k_lo[:, 0:4, :].bitcast(f32).rearrange("p a (c t) -> p a c t", c=HC)
        w13_sb = sb(ctx, "w13_sb", [P, 4, HC, FH])
        w2_sb = sb(ctx, "w2_sb", [P, FC, HID])
        w2_lo = sb(ctx, "w2_lo", [P, FC - 1, HID], f32r)
        xg = sb(ctx, "xg", [P, HID])
        xgT_hi = sb(ctx, "xgT_hi", [P, HC, P], f32r)
        xgT_lo = sb(ctx, "xgT_lo", [P, HC, P], f32r)
        gate = sb(ctx, "gate", [P, F])
        act = sb(ctx, "act", [P, F + 2 * FTAIL])
        actT_hi = sb(ctx, "actT_hi", [P, FC, P], f32r)
        actT_lo = sb(ctx, "actT_lo", [P, FC - 1, P], f32r)
        y_sb = sb(ctx, "y_sb", [P, HID])
        lmax = sb(ctx, "lmax", [P, NT])
        lsh = sb(ctx, "lsh", [P, NT, E])
        pe_ = sb(ctx, "pe_", [P, NT, E])
        psums = sb(ctx, "psums", [P, NT])
        prec = sb(ctx, "prec", [P, NT])
        pr = sb(ctx, "pr", [P, NT, E])
        top = sb(ctx, "top", [P, NT, E])
        top_i = sb(ctx, "top_i", [P, NT, E], u32)
        top_f = sb(ctx, "top_f", [P, NT, E])
        wsum = sb(ctx, "wsum", [P, NT])
        wrec = sb(ctx, "wrec", [P, NT])
        wtok = sb(ctx, "wtok", [P, TOPK, NT])
        pick = sb(ctx, "pick", [P, TOPK, NT, E])
        picks = sb(ctx, "picks", [P, NT, E], bf16)
        n_i = sb(ctx, "n_i", [P, E], i32)
        c_i = sb(ctx, "c_i", [P, E], i32)
        c_f = sb(ctx, "c_f", [P, E])
        c_bef = sb(ctx, "c_bef", [P, E, E])
        first = sb(ctx, "first", [P, E])
        ends = sb(ctx, "ends", [P, E])
        slot_e = sb(ctx, "slot_e", [P, NT, E])
        slot_p = sb(ctx, "slot_p", [P, TOPK, NT, E])
        slot_f = sb(ctx, "slot_f", [P, TOPK, NT])
        slot_i = sb(ctx, "slot_i", [P, TOPK, NT], i32)
        slot_row = sb(ctx, "slot_row", [P, TOPK, NT], i32)
        slot_tile = sb(ctx, "slot_tile", [P, TOPK, NT], i32)
        row_hot = sb(ctx, "row_hot", [P, TOPK, NT, P], bf16)
        tile_hot = sb(ctx, "tile_hot", [P, TOPK, NT, MT], bf16)
        parts = sb(ctx, "parts", [P, PARTS, TOPK, NT], bf16)
        of_slot = sb(ctx, "of_slot", [P, TOPK, NT, PARTS, MT], bf16)
        w_rest = sb(ctx, "w_rest", [P, 2, TOPK, NT])
        inv_parts = sb(ctx, "inv_parts", [P, PARTS, MT])
        inv = sb(ctx, "inv", [P, 2, MT])
        empty = sb(ctx, "empty", [P, MT])
        from_row = sb(ctx, "from_row", [P, MT], u32)
        to_row = sb(ctx, "to_row", [P, MT], u32)
        from_now = sb(ctx, "from_now", [P, 1], u32)
        to_now = sb(ctx, "to_now", [P, 1], u32)
        carrier = sb(ctx, "carrier", [P, 1])
        passed = sb(ctx, "passed", [P, MT, E])
        tile_f = sb(ctx, "tile_f", [P, MT])
        tile_i = sb(ctx, "tile_i", [P, MT], i32)
        more_i = sb(ctx, "more_i", [P, 1], i32)
        new_f = sb(ctx, "new_f", [P, MT])
        new_i = sb(ctx, "new_i", [P, MT], i32)

        ps4 = ctx.enter_context(nc.psum_tensor("ps4", [P, 4, 512], f32))
        ps2 = ctx.enter_context(nc.psum_tensor("ps2", [P, 2, 512], f32))
        ps_o = ctx.enter_context(nc.psum_tensor("ps_o", [P, 512], f32))
        ps_m = ctx.enter_context(nc.psum_tensor("ps_m", [P, 512], f32))
        banks = [ps4[:, i, :] for i in range(4)] + [ps2[:, i, :] for i in range(2)] + [ps_o[:, :], ps_m[:, :]]
        NB = len(banks)

        s_x = [sem(f"s_x{b}") for b in range(B)]
        s_x_more = sem("s_x_more")
        s_w = [sem(f"s_w{n}") for n in "qkv"]
        s_wh, s_wl = sem("s_wh"), sem("s_wl")
        s_wo, s_gw = sem("s_wo"), sem("s_gw")
        s_const = sem("s_const")
        s_dve = sem("s_dve")
        s_var, s_std = sem("s_var"), sem("s_std")
        s_xn = sem("s_xn")
        s_job = sem("s_job")
        s_ja = sem("s_ja")
        s_jd = sem("s_jd")
        s_stack = [sem(f"s_stack{r}") for r in range(RING)]
        s_row = [sem(f"s_row{r}") for r in range(4)]
        s_ones = sem("s_ones")
        s_sn = sem("s_sn")
        s_mx = sem("s_mx")
        s_mt = sem("s_mt")
        s_mr = sem("s_mr")
        s_st = sem("s_st")
        s_ex = sem("s_ex")
        s_pv = sem("s_pv")
        s_or = sem("s_or")
        s_so = [sem(f"s_so{r}") for r in range(2)]
        s_rc = sem("s_rc")
        s_rb = sem("s_rb")
        s_sh = sem("s_sh")
        s_on = sem("s_on")
        s_oc = [sem(f"s_oc{r}") for r in range(2)]
        s_zero, s_zt = sem("s_zero"), sem("s_zt")
        s_tail = sem("s_tail")
        s_init = sem("s_init")
        s_rows = sem("s_rows")
        s_hot, s_inv, s_where = sem("s_hot"), sem("s_inv"), sem("s_where")
        s_op, s_res, s_xn2, s_t2, s_t2e, s_lg = (sem(n) for n in ("s_op", "s_res", "s_xn2", "s_t2", "s_t2e", "s_lg"))
        s_lsh, s_lex, s_pick, s_rank, s_slot = (sem(n) for n in ("s_lsh", "s_lex", "s_pick", "s_rank", "s_slot"))
        s_w13 = [sem(f"s_w13_{q}") for q in range(4)]
        s_w2 = sem("s_w2")
        s_hi13, s_lo13 = sem("s_hi13"), sem("s_lo13")
        s_lo13p = sem("s_lo13p")
        s_hi2 = sem("s_hi2")
        s_lo2 = [sem(f"s_lo2_{h}") for h in range(3)]
        s_xg, s_xt, s_xh, s_xl = (sem(n) for n in ("s_xg", "s_xt", "s_xh", "s_xl"))
        s_up, s_silu, s_act = (sem(n) for n in ("s_up", "s_silu", "s_act"))
        s_at, s_ah, s_al = (sem(n) for n in ("s_at", "s_ah", "s_al"))
        s_down, s_ye, s_add = (sem(n) for n in ("s_down", "s_ye", "s_add"))
        s_now = sem("s_now")
        N_CONST = 11

        jobs = []
        for b in range(B):
            jobs += [("t", b, i) for i in range(TPB)]
            jobs += [(kind, b, i) for kind in "qk" for i in range(HC)]
            jobs += [("v", b, i) for i in range(TPB)]
        n_of = {j: n for n, j in enumerate(jobs)}
        a_count = [n + 1 for n in range(len(jobs))]
        d_count, c = [], 0
        for j in jobs:
            c += j[0] in "tqk"
            d_count.append(c)

        nj = len(jobs) // B
        bank_of = [n % NB for n in range(nj)] + [(0, 1, 2, 3, 6)[n % 5] for n in range(nj)]
        job_bank = [banks[k] for k in bank_of]
        early = [divmod(n, 4 * TPB) for n in range(8 * TPB)]
        between = [[early.pop(0) for _ in range(0 if n < TPB - 1 else 2 + n % 2) if early] for n in range(nj)]

        def job_read(eng, n):
            if jobs[n][0] in "tqk":
                eng.wait_ge(s_jd, d_count[n])
            eng.wait_ge(s_ja, a_count[n])

        def head_at(g, j):
            at = (g // 2) % RING
            return qs[at][:, j % 2, 2 * (g % 2) + j // 2, :], ks[at][:, 2 * (g % 2) + j // 2, :]

        def scores_at(u2):
            j, qt = divmod(u2, TPB)
            return j, qt, (j % 2) * 8 + (j // 2) * TPB + qt

        turns = []
        for s in range(-2, NG):
            turns += [(s + 2, u2) for u2 in range(2)]
            turns += [(s + 1, "maxima")] * (s + 1 >= 0)
            turns += [(s + 2, u2) for u2 in range(2, 4 * TPB)]
        turns = [t for t in turns if t[0] < NG]
        turns += [(t, "projection") for t in range(TPB)] + [(t, "router") for t in range(NT)]
        max_banks = [ps2[:, 0, :], ps2[:, 1, :], ps_m[:, :]]
        turn_of = {t: n for n, t in enumerate(turns)}

        def tiles_taken(eng):
            eng.wait_ge(s_slot, 1)
            return eng.value_load(more_i[0:1, 0:1], min_val=0, max_val=MT - LT) + LT

        def max_bank(g, what):
            return max_banks[turn_of[g, what] % 3]

        def max_bank_free(eng, g, what):
            n = turn_of[g, what] - 3
            if n >= 0:
                before, what = turns[n]
                if what in ("maxima", "projection", "router"):
                    eng.wait_ge({"maxima": s_mr, "projection": s_res, "router": s_t2e}[what], before + 1)
                else:
                    eng.wait_ge(s_mx, before * 16 + what + 1)

        block = ctx.enter_context(nc.Block())

        @block.sync
        def _(sp):
            x_t = x.rearrange("(n p) h -> p n h", p=P)
            for half, done in ((0, s_x[0]), (1, s_x_more)):
                at = slice(half * TPB // 2, (half + 1) * TPB // 2)
                sp.dma_start(x_sb[:, at, :], x_t[:, at, :]).then_inc(done, 16)
            for to, w, done in zip(w_raw, (wq, wk, wv), s_w):
                sp.dma_start(to, w.rearrange("p (c e) -> p c e", c=HC)).then_inc(done, 16)
            sp.dma_start(x_sb[:, TPB:NT, :], x_t[:, TPB:NT, :]).then_inc(s_x[1], 16)
            sp.wait_ge(s_zero, 3)
            sp.dma_start(out[T:T + P, :], rec_row[:, :]).then_inc(s_init, 16)

            def ready(pair):
                if pair != 1:
                    sp.wait_ge(s_ones, 2 * min(pair + 1, RING))
                if pair >= RING:
                    sp.wait_ge(s_st, UNITS * (2 * (pair - RING) + 2))
                sp.wait_ge(s_jd, d_count[n_of["k", pair // HC, pair % HC]])

            def stack(pair, pars, kinds):
                at = pair % RING
                for par in pars:
                    for part, (qsrc, ksrc) in enumerate(((q_hi, k_hi), (q_lo, k_hi), (q_hi, k_lo))):
                        dst = slice(64 * par + D * part, 64 * par + D * (part + 1))
                        for kind in kinds:
                            to, frm = (qs[at][dst, par, :, :], qsrc) if kind == "q" else (ks[at][dst, :, :], ksrc)
                            sp.dma_start(to.bitcast(f32),
                                         frm[64 * par:64 * par + 64, pair, :].bitcast(f32)).then_inc(s_stack[at], 16)

            for s in range(-4, NG + 2):
                g = s + 1
                if 0 <= g < NG:
                    sp.wait_ge(s_mr, g + 1)
                    for par in range(2):
                        sp.dma_start(qs[(g // 2) % RING][MROW:MROW + 1, par, 2 * (g % 2):2 * (g % 2) + 2, :].bitcast(f32)
                                     .rearrange("a p (t c) -> a (p t) c", c=P),
                                     max_rows[8 * par:8 * par + 8, g % 2, :].bitcast(f32)).then_inc(s_row[g % 4], 16)
                g = s - 2
                if 0 <= g < NG:
                    sp.wait_ge(s_rc, g + 1)
                    if g >= 1:
                        sp.wait_ge(s_sh, g)
                    sp.dma_start(rec_row[1:P:2 * D, :], sum_rec[:, g % 2, :]).then_inc(s_rb, 16)
                g = s - 1
                if 0 <= g < NG:
                    sp.wait_ge(s_or, g + 1)
                    if g >= 2:
                        sp.wait_ge(s_rb, 16 * (g - 1))
                    sp.dma_start(sum_rec[:, g % 2, :], o_raw[1:P:2 * D, g % 2, :]).then_inc(s_so[g % 2], 16)
                if s in (-4, -3) or s >= 0:
                    pair = (s + 4) // 2
                    if pair < NG // 2:
                        if s % 2 == 0:
                            ready(pair)
                        stack(pair, [s % 2], "qk")
                elif s == -2:
                    sp.wait_ge(s_ones, 3)
                    ready(1)
                    stack(1, range(2), "q")
                elif s == -1:
                    sp.wait_ge(s_ones, 4)
                    stack(1, range(2), "k")
                g = s - 2
                if g >= 0:
                    sp.wait_ge(s_on, g + 1)
                    sp.dma_start(o_all[64 * (g % 2):64 * (g % 2) + 64, g // 2, :],
                                 o_norm[0:P:2, g % 2, :]).then_inc(s_oc[g % 2], 16)
                if g == 8:
                    sp.dma_start(wo_sb, wo.rearrange("p (c e) -> p c e", c=HC)).then_inc(s_wo, 16)
                    sp.dma_start(gw_sb[:, :, :], gw.rearrange("p (c e) -> p c e", c=HC)).then_inc(s_gw, 16)
                if s in (NG - 2, NG - 1):
                    b = s - (NG - 2)
                    sp.wait_ge(s_st, UNITS * (NG - 2))
                    sp.dma_start(x1[:, b * TPB:(b + 1) * TPB, :], x_t[:, b * TPB:(b + 1) * TPB, :]).then_inc(s_x[b], 16)
            sp.wait_ge(s_pv, TPB * NG)
            sp.wait_ge(s_on, NG)

            def of_tile(i):
                return (sp.value_load(tile_i[0:1, bass.ds(i, 1)], min_val=0, max_val=E - 1),
                        sp.value_load(new_i[0:1, bass.ds(i, 1)], min_val=0, max_val=1))

            W13 = HC * FH

            def load13(q, e, cond):
                sp.dma_start(w13_sb[:, q, :, :].rearrange("p c f -> p (c f)"),
                             w13[bass.ds(e, 1), :, q * W13:(q + 1) * W13].rearrange("a p n -> (a p) n"),
                             cond=cond).then_inc(s_w13[q], 16)

            def load2(e, cond):
                sp.dma_start(w2_sb[:, 0:FC - 1, :].rearrange("p c f -> p (c f)"),
                             w2[bass.ds(e, 1), :, :].rearrange("a p n -> (a p) n"), cond=cond).then_inc(s_w2, 16)
                sp.dma_start(w2_sb[0:STACK, FC - 1, :],
                             w2t[bass.ds(e, 1), :, :].broadcast_to([3, FTAIL, HID]), cond=cond).then_inc(s_w2, 16)

            def ahead13(i):
                e, new = of_tile(i)
                for q in range(4):
                    sp.wait_ge(s_lo13, 4 * i - 3 + q)
                    if q == 3:
                        sp.wait_ge(s_lo13p, i)
                    load13(q, e, new)

            def ahead2(i):
                e, new = of_tile(i)
                for h in range(3):
                    sp.wait_ge(s_lo2[h], i)
                load2(e, new)

            for q in range(4):
                load13(q, 0, None)
            sp.wait_ge(s_tail, 1)
            load2(0, None)
            for b in range(B):
                sp.wait_ge(s_xn2, TPB * (b + 1))
                sp.dma_start(xn2_dram.rearrange("(n p) h -> p n h", p=P)[:, b * TPB:(b + 1) * TPB, :],
                             xn2[:, b * TPB:(b + 1) * TPB, :]).then_inc(s_rows, 16)
            sp.dma_start(out[0:T, :].rearrange("(n p) h -> p n h", p=P), x1[:, :, :]).then_inc(s_init, 16)
            sp.wait_ge(s_slot, 1)
            e, new = of_tile(0)
            for q in range(4):
                sp.wait_ge(s_w13[q], 16)
            sp.wait_ge(s_w2, 32)
            for q in range(4):
                load13(q, e, new)
            load2(e, new)
            ahead13(1)
            ahead13(2)
            ahead2(1)
            n = tiles_taken(sp)
            with sp.Fori(1, MT - 2) as i:
                with sp.If(i < n - 2):
                    ahead13(i + 2)
                    ahead2(i + 1)
            ahead2(n - 1)

        @block.gpsimd
        def _(pool):
            pool.memset(ident[:, :], 0.0).then_inc(s_zero, 1)
            pool.memset(before_b[:, :], 1.0).then_inc(s_zero, 1)
            pool.memset(rec_row[:, :], 0.0).then_inc(s_zero, 1)
            pool.wait_ge(s_zero, 3)
            pool.affine_select(out=ident[:, :], in_=ident[:, :], compare_op=ALU.not_equal, fill=1.0,
                               base=0, pattern=[[-1, P]], channel_multiplier=1).then_inc(s_const, 1)
            pool.affine_select(out=before_b[:, :], in_=before_b[:, :], compare_op=ALU.is_gt, fill=0.0,
                               base=0, pattern=[[1, P]], channel_multiplier=-1).then_inc(s_const, 1)
            pool.memset(ones_b[:, :], 1.0).then_inc(s_const, 1)
            pool.memset(v_ones[:, :, :, :, 1], 1.0).then_inc(s_const, 1)

            def prepare(r):
                pool.memset(qs[r][:, :, :, :].bitcast(f32), 0.0).then_inc(s_ones, 1)
                pool.memset(ks[r][:, :, :].bitcast(f32), 1.0).then_inc(s_ones, 1)

            prepare(0)
            pool.iota(e_of[:, :, :], pattern=[[0, NT], [1, E]], base=0, channel_multiplier=0,
                      allow_small_or_imprecise_dtypes=True).then_inc(s_const, 1)
            pool.iota(tile_of[:, :, :], pattern=[[1, MT], [0, E]], base=0, channel_multiplier=0,
                      allow_small_or_imprecise_dtypes=True).then_inc(s_const, 1)
            pool.iota(row_i[:, :], pattern=[[1, P]], base=0, channel_multiplier=0).then_inc(s_const, 1)
            pool.iota(token_parts[:, 0, :, :], pattern=[[0, TOPK], [P, NT]], base=0, channel_multiplier=0,
                      allow_small_or_imprecise_dtypes=True).then_inc(s_const, 1)
            pool.iota(token_parts[:, 1, :, :], pattern=[[0, TOPK], [0, NT]], base=1, channel_multiplier=1,
                      allow_small_or_imprecise_dtypes=True).then_inc(s_const, 1)
            pool.iota(dump_1[:, :], pattern=[[0, 1]], base=T + 1, channel_multiplier=1,
                      allow_small_or_imprecise_dtypes=True).then_inc(s_const, 1)
            pool.memset(e_before[:, :, :], 1.0).then_inc(s_zt, 1)
            pool.wait_ge(s_zt, 1)
            pool.affine_select(out=e_before[:, :, :], in_=e_before[:, :, :], compare_op=ALU.is_gt, fill=0.0,
                               base=0, pattern=[[1, E], [-1, E]], channel_multiplier=0).then_inc(s_const, 1)
            pool.wait_ge(s_job, n_of["q", 1, HC - 1] + 1)
            pool.memset(q1[:, :, :, :].bitcast(f32), 0.0).then_inc(s_ones, 1)
            pool.wait_ge(s_job, n_of["k", 1, HC - 1] + 1)
            pool.memset(k1[:, :, :].bitcast(f32), 1.0).then_inc(s_ones, 1)
            pool.wait_ge(s_job, len(jobs))
            prepare(2)
            for g in range(NG):
                pool.wait_ge(s_sh, g + 1)
                if g >= 2:
                    pool.wait_ge(s_oc[g % 2], 16 * (g // 2))
                pool.tensor_tensor(o_norm[:, g % 2, :], o_raw[:, g % 2, :], rec_all[:, :],
                                   ALU.mult).then_inc(s_on, 1)
            pool.wait_ge(s_pv, TPB * NG)
            pool.memset(w2_sb[:, FC - 1, :], 0.0).then_inc(s_tail, 1)

            copies = [0]

            def copied():
                copies[0] += 1
                pool.wait_ge(s_now, copies[0])

            def number(now, rows, i):
                return pool.tensor_copy(now[:, :], rows[:, bass.ds(i, 1)]).then_inc(s_now, 1)

            def rows_in(at=from_now):
                pool.indirect_dma_start(
                    out=xg[:, :], out_offset=None, in_=xn2_dram[:, :],
                    in_offset=bass.IndirectOffsetOnAxis(ap=at[:, 0:1], axis=0)).then_inc(s_xg, 16)

            def add_rows():
                pool.indirect_dma_start(
                    out=out[:, :], out_offset=bass.IndirectOffsetOnAxis(ap=to_now[:, 0:1], axis=0),
                    in_=y_sb[:, :], in_offset=None, compute_op=ALU.add).then_inc(s_add, 16)

            def split2(c0, c1):
                return pool.tensor_tensor(w2_lo[:, c0:c1, :], w2_sb[:, c0:c1, :], w2_hi[:, c0:c1, :].bitcast(f32),
                                          ALU.subtract)

            def split13(i):
                pool.wait_ge(s_hi13, 4 * i + 4)
                c = HC - 1
                pool.tensor_tensor(w13_lo[:, 3, c, :], w13_sb[:, 3, c, :], w13_hi[:, 3, c, :].bitcast(f32),
                                   ALU.subtract).then_inc(s_lo13p, 1)

            pool.wait_ge(s_where, 1)
            pool.wait_ge(s_rows, 16 * B)
            for i in range(3):
                if i > 0:
                    pool.wait_ge(s_xt, i)
                    number(from_now, from_row, i)
                    copied()
                rows_in(from_now if i else from_row)
                if i < 2:
                    split13(i)
            pool.wait_ge(s_hi2, 2)
            split2(FC // 2, FC - 1).then_inc(s_lo2[1], 1)
            pool.wait_ge(s_where, 2)
            pool.wait_ge(s_init, 32)
            n = tiles_taken(pool)
            with pool.Fori(1, MT - 2) as i:
                with pool.If(i < n - 2):
                    pool.wait_ge(s_xt, i + 2)
                    number(from_now, from_row, i + 2)
                    number(to_now, to_row, i - 1)
                    pool.wait_ge(s_now, 2 * i + 2)
                    split13(i + 1)
                    rows_in()
                    pool.wait_ge(s_ye, i)
                    pool.wait_ge(s_hi2, 2 * i + 2)
                    split2(FC // 2, FC // 2 + 1)
                    add_rows()
                    split2(FC // 2 + 1, FC - 1).then_inc(s_lo2[1], 1)
                    pool.wait_ge(s_add, 16 * i)
            for k in range(3):
                i = n - 2 + k
                number(to_now, to_row, i - 1)
                pool.wait_ge(s_now, 2 * n - 3 + k)
                pool.wait_ge(s_ye, i)
                if k == 0:
                    split13(i + 1)
                if k < 2:
                    pool.wait_ge(s_hi2, 2 * i + 2)
                    split2(FC // 2, FC - 1).then_inc(s_lo2[1], 1)
                else:
                    pool.tensor_tensor(carrier[:, :], dump_1[:, :], dump_1[:, :], ALU.add)
                add_rows()
                pool.wait_ge(s_add, 16 * i)

        @block.tensor
        def _(pe):
            pe.wait_ge(s_const, 1)
            def three(o, x_hi, x_lo, w_hi, w_lo, start, stop):
                pe.matmul(o, x_hi, w_hi, start=start, stop=False)
                pe.matmul(o, x_hi, w_lo, start=False, stop=False)
                return pe.matmul(o, x_lo, w_hi, start=False, stop=stop)

            def pv(g, kc):
                if not 0 <= g < NG:
                    return
                pe.wait_ge(s_ex, UNITS * g + 2 * (kc + 1))
                if kc == 0 and g >= 1:
                    pe.wait_ge(s_or, g)
                for j in range(GH):
                    last = pe.matmul(ps_o[32 * j:32 * j + 32, :],
                                     v_ones[:, (g // 8) * TPB + kc, (g % 8) * GH + j, :, :].rearrange("p d o -> p (d o)"),
                                     probs_t[:, kc % 2, j, :], start=(kc == 0), stop=(kc == TPB - 1),
                                     tile_position=(0, 32 * j))
                last.then_inc(s_pv, 1)

            def max_t(g):
                pe.wait_ge(s_mx, 16 * (g + 1))
                max_bank_free(pe, g, "maxima")
                pe.transpose(max_bank(g, "maxima")[0:4 * GH, 0:P], neg_max[:, g % 2, :], ident[:, :]).then_inc(s_mt, 1)

            def key_max(g, u2):
                if g >= NG:
                    return
                j, qt, _ = scores_at(u2)
                q, k = head_at(g, j)
                max_bank_free(pe, g, u2)
                pe.matmul(max_bank(g, u2), q[0:MROW, qt * P:(qt + 1) * P],
                          k[0:MROW, :], start=True, stop=True).then_inc(s_sn, 1)

            def scores(g, u):
                if not 0 <= g < NG:
                    return
                n = g * UNITS + u
                if n >= 2:
                    pe.wait_ge(s_ex, n - 1)
                kc, half = divmod(u, 2)
                for c in range(2):
                    q, k = head_at(g, 2 * half + c)
                    last = pe.matmul(ps4[:, 2 * (n % 2) + c, :], k[0:MROW + 1, kc * P:(kc + 1) * P],
                                     q[0:MROW + 1, :], start=True, stop=True)
                last.then_inc(s_st, 1)

            for n, (kind, b, i) in enumerate(jobs):
                before = [m for m in range(n) if bank_of[m] == bank_of[n]]
                if before:
                    job_read(pe, before[-1])
                o = job_bank[n]
                if kind == "t":
                    pe.wait_ge(s_xn, b * TPB + i + 1)
                    for c in range(HC):
                        last = pe.transpose(o[:, c * P:(c + 1) * P], x_sb[:, b * TPB + i, c * P:(c + 1) * P], ident[:, :])
                else:
                    which = "qkv".index(kind)
                    pe.wait_ge(s_wl, which + 1)
                    pe.wait_ge(s_jd, d_count[n_of[("t", b, TPB - 1)]])
                    at = slice(i * P, (i + 1) * P)
                    for c in range(HC):
                        x2 = [t[:, c, :] for t in (xnT_hi, xnT_lo)]
                        w2 = [t[which][:, c, :] for t in (w_hi, w_lo)]
                        if kind == "v":
                            last = three(o, *(t[:, at] for t in x2), *w2, c == 0, c == HC - 1)
                        else:
                            last = three(o, *(t[:, at] for t in w2), *x2, c == 0, c == HC - 1)
                last.then_inc(s_job, 1)
                if b == 1:
                    if between[n - nj] and (0, 0) == between[n - nj][0]:
                        pe.wait_ge(s_ja, a_count[nj - 1])
                        pe.wait_ge(s_jd, d_count[nj - 1])
                        pe.wait_ge(s_stack[0], 16 * 12)
                    for g, u2 in between[n - nj]:
                        if (g, u2) == (1, 2):
                            max_t(0)
                        key_max(g, u2)
            pe.wait_ge(s_const, N_CONST)
            pe.wait_ge(s_ja, a_count[-1])
            pe.wait_ge(s_jd, d_count[-1])

            def project(o, t, c0, c1):
                b, qt = divmod(t, TPB)
                for c in range(c0, c1):
                    last = pe.matmul(o, o_all[:, b * HC + c, qt * P:(qt + 1) * P], wo_sb[:, c, :],
                                     start=(c == 0), stop=(c == HC - 1))
                return last

            def packed(n):
                for r in range(2):
                    pe.wait_ge(s_oc[r], 16 * n // 2)

            def projection(t):
                pe.wait_ge(s_wo, 16)
                packed(NG // B)
                max_bank_free(pe, t, "projection")
                project(max_bank(t, "projection"), t, 0, HC).then_inc(s_op, 1)

            for s in range(0, NG + 1):
                ga = s + 2
                if ga < NG and ga % 2 == 0:
                    pe.wait_ge(s_stack[(ga // 2) % RING], 16 * 12 * (ga // 2 // RING + 1))
                if 0 <= s < NG:
                    pe.wait_ge(s_row[s % 4], 32 * (s // 4 + 1))
                for p in range(TPB):
                    key_max(ga, 4 * p)
                    key_max(ga, 4 * p + 1)
                    if p < 2:
                        pv(s - 1, p + 2)
                    else:
                        pv(s, p - 2)
                    if p == 0 and 0 <= s + 1 < NG:
                        max_t(s + 1)
                    key_max(ga, 4 * p + 2)
                    scores(s, 2 * p)
                    key_max(ga, 4 * p + 3)
                    scores(s, 2 * p + 1)
                    if s in (NG - 2, NG - 1) and p == 1:
                        projection(s - (NG - 2))

            for t in range(2, TPB):
                projection(t)
            packed(NG - 2)
            pe.wait_ge(s_ex, UNITS * NG)
            for t in range(TPB, NT):
                project(ps4[:, t % TPB, :], t, 0, HC - 1)
            packed(NG)
            for t in range(TPB, NT):
                project(ps4[:, t % TPB, :], t, HC - 1, HC).then_inc(s_op, 1)
            pe.wait_ge(s_gw, 16)
            pe.wait_ge(s_or, NG)
            for b in range(B):
                tiles = range(b * TPB, (b + 1) * TPB)
                for t in tiles:
                    pe.wait_ge(s_xn2, t + 1)
                    max_bank_free(pe, t, "router")
                    o = max_bank(t, "router")
                    for c in range(HC):
                        last = pe.transpose(o[:, c * P:(c + 1) * P], xn2[:, t, c * P:(c + 1) * P], ident[:, :])
                    last.then_inc(s_t2, 1)
                for t in tiles:
                    pe.wait_ge(s_t2e, t + 1)
                    for c in range(HC):
                        last = pe.matmul(ps_o[:, t * E:(t + 1) * E], xn2T[:, t % TPB, c, :], gw_sb[:, c, :],
                                         start=(c == 0), stop=(c == HC - 1))
                    last.then_inc(s_lg, 1)
            pe.wait_ge(s_pick, 1)
            pk = picks[:, :, :].rearrange("p t e -> p (t e)")
            for d in range(1, NT):
                pe.matmul(ps_m[:, d * E:NT * E], ones_b[:, :], pk[:, 0:(NT - d) * E],
                          start=(d == 1), stop=False, skip_group_check=True)
            pe.matmul(ps_m[:, 0:NT * E], before_b[:, :], pk, start=False, stop=True, skip_group_check=True)
            for t in range(NT):
                last = pe.matmul(ps2[:, 0, 0:E], ones_b[:, :], pk[:, t * E:(t + 1) * E],
                                 start=(t == 0), stop=(t == NT - 1))
            last.then_inc(s_rank, 1)

            for k in range(TOPK):
                pe.wait_ge(s_hot, k + 1)
                for t in range(NT):
                    last = pe.matmul(ps4[:, 0, 0:PARTS * MT], row_hot[:, k, t, :],
                                     of_slot[:, k, t, :, :].rearrange("p a m -> p (a m)"),
                                     start=(k == 0 and t == 0), stop=(k == TOPK - 1 and t == NT - 1))
            last.then_inc(s_inv, 1)

            def rows_in(i):
                pe.wait_ge(s_xg, 16 * (i + 1))
                for c in range(HC):
                    last = pe.transpose(ps_m[:, c * P:(c + 1) * P], xg[:, c * P:(c + 1) * P], ident[:, :])
                last.then_inc(s_xt, 1)

            def up(i):
                pe.wait_ge(s_xl, i + 1)
                for q in range(4):
                    pe.wait_ge(s_lo13, 4 * i + q + 1)
                    if q == 3:
                        pe.wait_ge(s_lo13p, i + 1)
                    if not (isinstance(i, int) and i == 0) and q in (0, 2):
                        pe.wait_ge((s_silu, s_act)[q // 2], i)
                    for c in range(HC):
                        last = three(ps4[:, q, 0:FH], xgT_hi[:, c, :], xgT_lo[:, c, :], w13_hi[:, q, c, :],
                                     w13_lo[:, q, c, :], c == 0, c == HC - 1)
                    last.then_inc(s_up, 1)

            def down(i):
                pe.wait_ge(s_al, i + 1)
                if not (isinstance(i, int) and i == 0):
                    pe.wait_ge(s_ye, i)
                for c in range(FC):
                    if c in (0, FC // 2):
                        pe.wait_ge(s_lo2[c // (FC // 2)], i + 1)
                    if c < FC - 1:
                        last = three(ps_o[:, :], actT_hi[:, c, :], actT_lo[:, c, :], w2_hi[:, c, :],
                                     w2_lo[:, c, :], c == 0, False)
                    else:
                        pe.wait_ge(s_lo2[2], i + 1)
                        last = pe.matmul(ps_o[:, :], actT_hi[0:STACK, c, :], w2_hi[0:STACK, c, :],
                                         start=False, stop=True)
                    if c in (FC // 2 - 1, FC - 1):
                        last.then_inc(s_down, 1)

            def inner_t(i):
                pe.wait_ge(s_act, i + 1)
                for c in range(FC):
                    k = P if c < FC - 1 else STACK
                    last = pe.transpose(ps2[0:k, c // 4, (c % 4) * P:(c % 4 + 1) * P],
                                        act[:, c * P:c * P + k], ident[:, :])
                last.then_inc(s_at, 1)

            rows_in(0)
            up(0)
            rows_in(1)
            inner_t(0)
            n = tiles_taken(pe)
            with pe.Fori(1, MT - 1) as i:
                with pe.If(i < n - 1):
                    up(i)
                    rows_in(i + 1)
                    down(i - 1)
                    inner_t(i)
            up(n - 1)
            down(n - 2)
            inner_t(n - 1)
            down(n - 1)

        @block.scalar
        def _(a):
            def root(n, t0):
                a.wait_ge(s_var, n)
                a.activation(rstd[:, t0:t0 + TPB], rstd[:, t0:t0 + TPB], ACT.Sqrt).then_inc(s_std, 1)

            def weights(which):
                a.wait_ge(s_w[which], 16)
                a.activation(w_hi[which][:, :, :], w_raw[which], ACT.Copy).then_inc(s_wh, 1)

            def maxima(g):
                a.wait_ge(s_mt, g + 1)
                if g >= 2:
                    a.wait_ge(s_row[(g - 2) % 4], 32 * ((g - 2) // 4 + 1))
                a.activation(max_rows[:, g % 2, :], max_bank(g, "maxima")[0:4 * GH, 0:P], ACT.Copy).then_inc(s_mr, 1)

            root(1, 0)
            weights(0)
            for n, (kind, b, i) in enumerate(jobs):
                o = job_bank[n]
                if (kind, b, i) == ("q", 0, 0):
                    weights(1)
                    weights(2)
                    root(2, TPB)
                a.wait_ge(s_job, n + 1)
                if kind == "t":
                    a.activation(xnT_hi[:, :, i * P:(i + 1) * P], o.rearrange("p (c t) -> p c t", c=HC),
                                 ACT.Copy).then_inc(s_ja, 1)
                elif kind == "v":
                    a.activation(v_ones[:, b * TPB + i, :, :, 0], o.rearrange("p (h d) -> p h d", d=D),
                                 ACT.Copy).then_inc(s_ja, 1)
                else:
                    hi = q_hi if kind == "q" else k_hi
                    a.activation(hi[:, b * HC + i, :], o, ACT.Copy).then_inc(s_ja, 1)
                if b == 1 and (1, 2) in between[n - nj]:
                    maxima(0)
            for s in range(0, NG + 1):
                for u in range(UNITS):
                    g = s + 1
                    if u == 0 and g < NG:
                        maxima(g)
                    g = s - 1
                    if u == 2 and g >= 0:
                        a.wait_ge(s_pv, TPB * (g + 1))
                        if g >= 2:
                            a.wait_ge(s_so[g % 2], 16 * (g // 2))
                            a.wait_ge(s_on, g - 1)
                        a.activation(o_raw[:, g % 2, :], ps_o[:, :], ACT.Copy).then_inc(s_or, 1)
                    if 0 <= s < NG:
                        n = s * UNITS + u
                        kc, half = divmod(u, 2)
                        m = s * TPB + kc
                        if m >= 2 and half == 0:
                            a.wait_ge(s_pv, m - 1)
                        a.wait_ge(s_st, n + 1)
                        a.activation(probs_t[:, kc % 2, 2 * half:2 * half + 2, :], ps4[:, 2 * (n % 2):2 * (n % 2) + 2, :],
                                     ACT.Exp, scale=D ** -0.5).then_inc(s_ex, 1)
            for t in range(NT):
                if t % TPB == 0:
                    root(B + t // TPB + 1, t)
                a.wait_ge(s_t2, t + 1)
                if t >= TPB:
                    a.wait_ge(s_lg, t - TPB + 1)
                a.activation(xn2T[:, t % TPB, :, :], max_bank(t, "router").rearrange("p (c t) -> p c t", c=HC),
                             ACT.Copy).then_inc(s_t2e, 1)
            a.wait_ge(s_lsh, 1)
            a.activation(pe_[:, :, :], lsh[:, :, :], ACT.Exp).then_inc(s_lex, 1)

            def split13(i, q):
                a.wait_ge(s_w13[q], 16 * (i + 2))
                if not (isinstance(i, int) and i == 0):
                    a.wait_ge(s_up, 4 * i + q - 3)
                a.activation(w13_hi[:, q, :, :], w13_sb[:, q, :, :], ACT.Copy).then_inc(s_hi13, 1)

            def split2(i, h):
                a.wait_ge(s_w2, 32 * (i + 2))
                if not (isinstance(i, int) and i == 0):
                    a.wait_ge(s_down, 2 * i + h - 1)
                c = slice(FC // 2, FC) if h else slice(0, FC // 2)
                a.activation(w2_hi[:, c, :], w2_sb[:, c, :], ACT.Copy).then_inc(s_hi2, 1)

            def silu(i):
                a.wait_ge(s_up, 4 * i + 2)
                if not (isinstance(i, int) and i == 0):
                    a.wait_ge(s_act, i)
                a.activation(gate[:, :].rearrange("p (h f) -> p h f", h=2), ps4[:, 0:2, 0:FH],
                             ACT.Silu).then_inc(s_silu, 1)

            def rows_hi(i):
                a.wait_ge(s_xt, i + 1)
                if not (isinstance(i, int) and i == 0):
                    a.wait_ge(s_up, 4 * i)
                a.activation(xgT_hi[:, :, :].rearrange("p c t -> p (c t)"), ps_m[:, :], ACT.Copy).then_inc(s_xh, 1)

            def inner_hi(i):
                a.wait_ge(s_at, i + 1)
                if not (isinstance(i, int) and i == 0):
                    a.wait_ge(s_down, 2 * i)
                a.activation(actT_hi[:, 0:4, :].rearrange("p c t -> p (c t)"), ps2[:, 0, :], ACT.Copy)
                a.activation(actT_hi[:, 4:6, :].rearrange("p c t -> p (c t)"), ps2[:, 1, 0:2 * P], ACT.Copy)
                a.activation(actT_hi[0:STACK, FC - 1, :], ps2[0:STACK, 1, 2 * P:3 * P], ACT.Copy).then_inc(s_ah, 1)

            def y_out(i):
                a.wait_ge(s_down, 2 * i + 2)
                if not (isinstance(i, int) and i == 0):
                    a.wait_ge(s_add, 16 * i)
                a.activation(y_sb[:, :], ps_o[:, :], ACT.Copy, scale=inv[:, 1, bass.ds(i, 1)]).then_inc(s_ye, 1)

            for q in range(4):
                split13(0, q)
            rows_hi(0)
            split13(1, 0)
            split13(1, 1)
            silu(0)
            split13(1, 2)
            split13(1, 3)
            rows_hi(1)
            split2(0, 0)
            split2(0, 1)
            inner_hi(0)
            n = tiles_taken(a)
            with a.Fori(1, MT - 1) as i:
                with a.If(i < n - 1):
                    split13(i + 1, 0)
                    split13(i + 1, 1)
                    silu(i)
                    split13(i + 1, 2)
                    split13(i + 1, 3)
                    rows_hi(i + 1)
                    split2(i, 0)
                    y_out(i - 1)
                    split2(i, 1)
                    inner_hi(i)
            silu(n - 1)
            split2(n - 1, 0)
            y_out(n - 2)
            split2(n - 1, 1)
            inner_hi(n - 1)
            y_out(n - 1)

        @block.vector
        def _(v):
            chain, norms = [0], [0]

            def link(ins):
                chain[0] += 1
                ins.then_inc(s_dve, 1)
                v.wait_ge(s_dve, chain[0])

            def norm(src, dst, t0, n, done, half=None):
                for t in range(t0, t0 + n):
                    if half is not None and t == t0 + n // 2:
                        v.wait_ge(half, 16)
                    ins = v.bn_stats(stats[:, t, :], src[:, t, :])
                link(ins)
                for t in range(t0, t0 + n):
                    ins = v.bn_aggr(aggr[:, t, :], stats[:, t, :])
                link(ins)
                v.tensor_scalar(rstd[:, t0:t0 + n], aggr[:, t0:t0 + n, 1], EPS, None, ALU.add).then_inc(s_var, 1)
                norms[0] += 1
                v.wait_ge(s_std, norms[0])
                link(v.reciprocal(rstd[:, t0:t0 + n], rstd[:, t0:t0 + n]))
                for k in range(n):
                    t = t0 + k
                    v.tensor_scalar(dst(t), src[:, t, :], aggr[:, t, 0:1], rstd[:, t:t + 1],
                                    ALU.subtract, ALU.mult).then_inc(done, 1)

            def weights(which):
                v.wait_ge(s_wh, which + 1)
                v.tensor_tensor(w_lo[which][:, :, :], w_raw[which], w_hi[which][:, :, :].bitcast(f32),
                                ALU.subtract).then_inc(s_wl, 1)

            def norm_x(b):
                v.wait_ge(s_x[b], 16)
                norm(x_sb, lambda t: x_sb[:, t, :], b * TPB, TPB, s_xn, None if b else s_x_more)

            def maximum(g, u2):
                _, _, col = scores_at(u2)
                v.wait_ge(s_sn, g * 16 + u2 + 1)
                v.tensor_reduce(neg_max[:, g % 2, col:col + 1], max_bank(g, u2), AX.X, ALU.max,
                                negate=True).then_inc(s_mx, 1)

            norm_x(0)
            weights(0)
            for n, (kind, b, i) in enumerate(jobs):
                if (kind, b, i) == ("q", 0, 0):
                    weights(1)
                    weights(2)
                    norm_x(1)
                if kind == "t":
                    v.wait_ge(s_ja, a_count[n])
                    at = slice(i * P, (i + 1) * P)
                    v.tensor_tensor(xnT_lo[:, :, at], job_bank[n].rearrange("p (c t) -> p c t", c=HC),
                                    xnT_hi[:, :, at].bitcast(f32), ALU.subtract).then_inc(s_jd, 1)
                elif kind in "qk":
                    hi, lo = (q_hi, q_lo) if kind == "q" else (k_hi, k_lo)
                    v.wait_ge(s_ja, a_count[n])
                    v.tensor_tensor(lo[:, b * HC + i, :], job_bank[n], hi[:, b * HC + i, :].bitcast(f32),
                                    ALU.subtract).then_inc(s_jd, 1)
                if b == 1:
                    for g, u2 in between[n - nj]:
                        maximum(g, u2)
            def residual(t):
                v.wait_ge(s_x[t // TPB], 32)
                v.wait_ge(s_op, t + 1)
                o = max_bank(t, "projection") if t < TPB else ps4[:, t % TPB, :]
                v.tensor_tensor(x1[:, t, :], o, x1[:, t, :], ALU.add).then_inc(s_res, 1)

            for s in range(0, NG + 2):
                ga = s + 2
                if ga < NG:
                    v.wait_ge(s_mt, ga - 1)
                for u2 in range(16):
                    if ga < NG:
                        maximum(ga, u2)
                    g = s - 2
                    if u2 == 1 and g >= 0:
                        v.wait_ge(s_so[g % 2], 16 * (g // 2 + 1))
                        v.reciprocal(sum_rec[:, g % 2, :], sum_rec[:, g % 2, :]).then_inc(s_rc, 1)
                        if s in (NG - 1, NG):
                            residual(s - (NG - 1))
                    if u2 == 11 and g >= 0:
                        v.wait_ge(s_rb, 16 * (g + 1))
                        if g >= 1:
                            v.wait_ge(s_on, g)
                        v.stream_shuffle(rec_all[:, :], rec_row[:, :], [1] * 32).then_inc(s_sh, 1)
            for b in range(B):
                for t in range(b * TPB, (b + 1) * TPB):
                    if t >= 2:
                        residual(t)
                v.wait_ge(s_res, (b + 1) * TPB)
                norm(x1, lambda t: xn2[:, t, :], b * TPB, TPB, s_xn2)
            v.wait_ge(s_lg, NT)
            v.wait_ge(s_const, N_CONST)
            lg = ps_o[:, 0:NT * E].rearrange("p (t e) -> p t e", e=E)
            wide = lambda a: a.unsqueeze(2).broadcast_to([P, NT, E])
            link(v.tensor_reduce(lmax[:, :], lg, AX.X, ALU.max))
            v.tensor_tensor(lsh[:, :, :], lg, wide(lmax[:, :]), ALU.subtract).then_inc(s_lsh, 1)
            v.wait_ge(s_lex, 1)
            link(v.tensor_reduce(psums[:, :], pe_[:, :, :], AX.X, ALU.add))
            link(v.reciprocal(prec[:, :], psums[:, :]))
            link(v.tensor_tensor(pr[:, :, :], pe_[:, :, :], wide(prec[:, :]), ALU.mult))
            for t in range(NT):
                ins = v.max(top[:, t, :], pr[:, t, :])
            link(ins)
            for t in range(NT):
                ins = v.max_index(top_i[:, t, :], top[:, t, :], pr[:, t, :])
            link(ins)
            v.tensor_reduce(wsum[:, :], top[:, :, 0:TOPK], AX.X, ALU.add)
            link(v.tensor_copy(top_f[:, :, :], top_i[:, :, :]))
            v.reciprocal(wrec[:, :], wsum[:, :])
            for k in range(TOPK):
                ins = v.tensor_tensor(pick[:, k, :, :], e_of[:, :, :], wide(top_f[:, :, k]), ALU.is_equal)
            link(ins)
            v.tensor_tensor(picks[:, :, :], pick[:, 0, :, :], pick[:, 1, :, :], ALU.add).then_inc(s_pick, 1)
            for k in range(TOPK):
                ins = v.tensor_tensor(wtok[:, k, :], top[:, :, k], wrec[:, :], ALU.mult)
            link(ins)
            v.tensor_copy(parts[:, 0:2, :, :], token_parts[:, :, :, :])
            link(v.tensor_copy(parts[:, 2, :, :], wtok[:, :, :]))
            link(v.tensor_tensor(w_rest[:, 0, :, :], wtok[:, :, :], parts[:, 2, :, :], ALU.subtract))
            link(v.tensor_copy(parts[:, 3, :, :], w_rest[:, 0, :, :]))
            link(v.tensor_tensor(w_rest[:, 1, :, :], w_rest[:, 0, :, :], parts[:, 3, :, :], ALU.subtract))
            v.tensor_copy(parts[:, 4, :, :], w_rest[:, 1, :, :])
            v.wait_ge(s_rank, 1)
            link(v.tensor_scalar(n_i[:, :], ps2[:, 0, 0:E], float(P - 1), None, ALU.add))
            link(v.tensor_scalar(c_i[:, :], n_i[:, :], 7, None, ALU.arith_shift_right))
            link(v.tensor_copy(c_f[:, :], c_i[:, :]))
            link(v.tensor_tensor(c_bef[:, :, :], e_before[:, :, :],
                                 c_f[:, :].unsqueeze(1).broadcast_to([P, E, E]), ALU.mult))
            link(v.tensor_reduce(first[:, :], c_bef[:, :, :], AX.X, ALU.add))
            v.scalar_tensor_tensor(slot_e[:, :, :], first[:, :].unsqueeze(1).broadcast_to([P, NT, E]), float(P),
                                   ps_m[:, 0:NT * E].rearrange("p (t e) -> p t e", e=E), ALU.mult, ALU.add)
            link(v.tensor_tensor(ends[:, :], first[:, :], c_f[:, :], ALU.add))
            for k in range(TOPK):
                v.tensor_tensor(slot_p[:, k, :, :], pick[:, k, :, :], slot_e[:, :, :], ALU.mult)
            link(v.tensor_tensor(passed[:, :, :], ends[:, :].unsqueeze(1).broadcast_to([P, MT, E]),
                                 tile_of[:, :, :], ALU.is_le))
            v.tensor_reduce(slot_f[:, :, :], slot_p[:, :, :, :], AX.X, ALU.add)
            link(v.tensor_reduce(tile_f[:, :], passed[:, :, :], AX.X, ALU.add))
            link(v.tensor_scalar(tile_f[:, :], tile_f[:, :], float(E - 1), None, ALU.min))
            v.tensor_copy(tile_i[:, :], tile_f[:, :])
            v.tensor_scalar(more_i[:, :], ends[:, E - 1:E], float(-LT), None, ALU.add)
            v.tensor_copy(new_f[:, 0:1], tile_f[:, 0:1])
            link(v.tensor_tensor(new_f[:, 1:MT], tile_f[:, 1:MT], tile_f[:, 0:MT - 1], ALU.subtract))
            v.tensor_scalar(new_i[:, :], new_f[:, :], 0.0, None, ALU.is_gt).then_inc(s_slot, 1)
            link(v.tensor_copy(slot_i[:, :, :], slot_f[:, :, :]))
            v.tensor_scalar(slot_row[:, :, :], slot_i[:, :, :], P - 1, None, ALU.bitwise_and)
            link(v.tensor_scalar(slot_tile[:, :, :], slot_i[:, :, :], 7, None, ALU.arith_shift_right))
            tiles = tile_of[:, :, 0].unsqueeze(1).broadcast_to([P, NT, MT])
            for k in range(TOPK):
                ins = v.tensor_tensor(tile_hot[:, k, :, :], tiles, slot_tile[:, k, :].unsqueeze(2).broadcast_to([P, NT, MT]),
                                      ALU.is_equal)
            link(ins)
            for k in range(TOPK):
                for n in range(PARTS):
                    v.tensor_tensor(of_slot[:, k, :, n, :], tile_hot[:, k, :, :],
                                    parts[:, n, k, :].unsqueeze(2).broadcast_to([P, NT, MT]), ALU.mult)
                v.tensor_tensor(row_hot[:, k, :, :], row_i[:, :].unsqueeze(1).broadcast_to([P, NT, P]),
                                slot_row[:, k, :].unsqueeze(2).broadcast_to([P, NT, P]), ALU.is_equal).then_inc(s_hot, 1)
            def split13(i, q):
                v.wait_ge(s_hi13, 4 * i + q + 1)
                if not (isinstance(i, int) and i == 0):
                    v.wait_ge(s_up, 4 * i + q - 3)
                c = slice(0, HC - (q == 3))
                v.tensor_tensor(w13_lo[:, q, c, :], w13_sb[:, q, c, :], w13_hi[:, q, c, :].bitcast(f32),
                                ALU.subtract).then_inc(s_lo13, 1)

            v.wait_ge(s_inv, 1)
            link(v.tensor_copy(inv_parts[:, :, :].rearrange("p a m -> p (a m)"), ps4[:, 0, 0:PARTS * MT]))
            v.tensor_tensor(inv[:, 1, :], inv_parts[:, 2, :], inv_parts[:, 3, :], ALU.add)
            link(v.tensor_tensor(inv[:, 0, :], inv_parts[:, 0, :], inv_parts[:, 1, :], ALU.add))
            v.tensor_scalar(from_row[:, :], inv[:, 0, :], -1.0, 0.0, ALU.add, ALU.max).then_inc(s_where, 1)
            v.tensor_tensor(inv[:, 1, :], inv[:, 1, :], inv_parts[:, 4, :], ALU.add)
            link(v.tensor_scalar(empty[:, :], inv[:, 0, :], 0.0, dump_1[:, 0:1], ALU.is_equal, ALU.mult))
            v.scalar_tensor_tensor(to_row[:, :], inv[:, 0, :], -1.0, empty[:, :], ALU.add, ALU.add).then_inc(s_where, 1)

            def split2(i):
                v.wait_ge(s_hi2, 2 * i + 1)
                if not (isinstance(i, int) and i == 0):
                    v.wait_ge(s_down, 2 * i - 1)
                v.tensor_tensor(w2_lo[:, 0:FC // 2, :], w2_sb[:, 0:FC // 2, :], w2_hi[:, 0:FC // 2, :].bitcast(f32),
                                ALU.subtract).then_inc(s_lo2[0], 1)

            def split_short(i):
                v.wait_ge(s_hi2, 2 * i + 2)
                at = slice(FTAIL, 2 * FTAIL)
                v.tensor_tensor(w2_hi[at, FC - 1, :], w2_sb[at, FC - 1, :], w2_hi[at, FC - 1, :].bitcast(f32),
                                ALU.subtract).then_inc(s_lo2[2], 1)

            def rows_lo(i):
                v.wait_ge(s_xh, i + 1)
                if not (isinstance(i, int) and i == 0):
                    v.wait_ge(s_up, 4 * i)
                v.tensor_tensor(xgT_lo[:, :, :].rearrange("p c t -> p (c t)"), ps_m[:, :],
                                xgT_hi[:, :, :].rearrange("p c t -> p (c t)").bitcast(f32), ALU.subtract).then_inc(s_xl, 1)

            def gated(i):
                v.wait_ge(s_silu, i + 1)
                v.wait_ge(s_up, 4 * i + 4)
                if not (isinstance(i, int) and i == 0):
                    v.wait_ge(s_at, i)
                v.tensor_tensor(act[:, 0:F].rearrange("p (h f) -> p h f", h=2), gate[:, :].rearrange("p (h f) -> p h f", h=2),
                                ps4[:, 2:4, 0:FH], ALU.mult)
                twice = lambda t: t.unsqueeze(1).broadcast_to([P, 2, FTAIL])
                v.tensor_tensor(act[:, F:F + 2 * FTAIL].rearrange("p (n f) -> p n f", n=2), twice(gate[:, F - FTAIL:F]),
                                twice(ps4[:, 3, FH - FTAIL:FH]), ALU.mult).then_inc(s_act, 1)

            def inner_lo(i):
                v.wait_ge(s_ah, i + 1)
                if not (isinstance(i, int) and i == 0):
                    v.wait_ge(s_down, 2 * i)
                for c0, c1, bank in ((0, 4, 0), (4, 6, 1)):
                    v.tensor_tensor(actT_lo[:, c0:c1, :].rearrange("p c t -> p (c t)"), ps2[:, bank, 0:(c1 - c0) * P],
                                    actT_hi[:, c0:c1, :].rearrange("p c t -> p (c t)").bitcast(f32), ALU.subtract)
                at = slice(2 * FTAIL, STACK)
                v.tensor_tensor(actT_hi[at, FC - 1, :], ps2[at, 1, 2 * P:3 * P],
                                actT_hi[at, FC - 1, :].bitcast(f32), ALU.subtract).then_inc(s_al, 1)

            for q in range(3):
                split13(0, q)
            rows_lo(0)
            split13(0, 3)

            def step(i, more=True):
                if more:
                    for q in range(3):
                        split13(i + 1, q)
                gated(i)
                if more:
                    rows_lo(i + 1)
                    split13(i + 1, 3)
                split2(i)
                inner_lo(i)
                split_short(i)

            step(0)
            n = tiles_taken(v)
            with v.Fori(1, MT - 1) as i:
                with v.If(i < n - 1):
                    step(i)
            step(n - 1, more=False)


def kernel(L0_attn_x, L0_attn_w_q, L0_attn_w_k, L0_attn_w_v, L0_attn_w_o,
           L0_ffn_gate_w, L0_ffn_w1, L0_ffn_w2, L0_ffn_w3):
    import numpy as np
    import concourse.bacc as bacc
    from concourse.bass_utils import run_bass_kernel_spmd

    def rows_first(w_t):
        r, n = w_t.shape
        return np.ascontiguousarray(w_t.reshape(r // P, P, n).transpose(1, 0, 2).reshape(P, -1))

    order = np.array([(8 * c + 4 * half + 2 * p + par) * D + d for c in range(HC)
                      for par in range(2) for d in range(D) for half in range(2) for p in range(2)])
    w1, w2, w3 = (np.asarray(w) for w in (L0_ffn_w1, L0_ffn_w2, L0_ffn_w3))
    w13 = np.concatenate([w1, w3], axis=1).transpose(0, 2, 1)
    w13 = np.ascontiguousarray(w13.reshape(E, HC, P, 4, FH).transpose(0, 2, 3, 1, 4).reshape(E, P, -1))
    w2_t = w2.transpose(0, 2, 1)
    main = (FC - 1) * P
    w2_main = np.ascontiguousarray(
        w2_t[:, :main, :].reshape(E, FC - 1, P, HID).transpose(0, 2, 1, 3).reshape(E, P, -1))
    arrays = {
        "x": np.asarray(L0_attn_x).reshape(T, HID),
        "wq": rows_first(np.asarray(L0_attn_w_q).T[:, order]),
        "wk": rows_first(np.asarray(L0_attn_w_k).T[:, order]),
        "wv": rows_first(np.asarray(L0_attn_w_v).T),
        "wo": rows_first(np.asarray(L0_attn_w_o).T),
        "gw": rows_first(np.asarray(L0_ffn_gate_w).T),
        "w13": w13,
        "w2": w2_main,
        "w2t": np.ascontiguousarray(w2_t[:, main:, :]),
    }
    nc = bacc.Bacc("TRN2", target_bir_lowering=False, num_devices=1)
    args = [nc.dram_tensor(k, a.shape, mybir.dt.from_np(a.dtype), kind="ExternalInput").ap() for k, a in arrays.items()]
    args.append(nc.dram_tensor("out", (T + P, HID), mybir.dt.float32, kind="ExternalOutput").ap())
    moe_layer(nc, *args)
    r = run_bass_kernel_spmd(nc, [arrays], core_ids=[0])
    return r.results[0]["out"][:T].reshape(B, S, HID)
```
